# Optimizing a Trainium2 kernel written in Bass

```python
import numpy as np
import jax
import jax.numpy as jnp

def _softmax(x, axis=-1):
    return jax.nn.softmax(x, axis=axis)

def _gelu(x):
    return jax.nn.gelu(x, approximate=True)

def _silu(x):
    return jax.nn.silu(x)

def _sigmoid(x):
    return jax.nn.sigmoid(x)

def _layernorm(x, axis=-1, eps=1e-05):
    m = jnp.mean(x, axis=axis, keepdims=True)
    v = jnp.var(x, axis=axis, keepdims=True)
    return (x - m) / jnp.sqrt(v + eps)

def _scatter_add(tgt, idx, src, axis=0):
    return tgt.at[idx].add(src)

def _segment_sum(src, seg, n):
    return jax.ops.segment_sum(src, seg, n)
kernel_name = 'mk_adj_resnorm_d2_adj_r2_e4015d'

def setup_inputs(seed: int=0):
    np.random.seed(seed)
    _w = jnp.asarray

    def _rec_inputs():
        import jax
        import jax.numpy as jnp
        _gk = jax.random.key(seed)
        x = -0.0001538 + 1 * jax.random.normal(jax.random.fold_in(_gk, 1), (128, 128, 384), jnp.float32)
        _a = jax.random.bernoulli(jax.random.fold_in(_gk, 2), 0.03125, (128, 128, 128))
        _a = jnp.logical_or(_a, jnp.swapaxes(_a, -1, -2))
        _a = jnp.logical_or(_a, jnp.eye(128, dtype=bool))
        _af = _a.astype(jnp.float32)
        _af = _af * jax.random.uniform(jax.random.fold_in(_gk, 3), (128, 128, 128), jnp.float32, 0.05, 4.42607)
        adj = _af
        return (x, adj)
    x, adj = _rec_inputs()

    def _L0_gnn_setup():
        import jax, jax.numpy as jnp
        import numpy as np
        NUM_HEADS = 12
        HIDDEN = 384
        HEAD = HIDDEN // NUM_HEADS
        B, N = (16, 256)
        key = jax.random.key(seed)
        ks = jax.random.split(key, 9)
        s = 0.02
        return {'x': jax.random.normal(ks[0], (B, N, HIDDEN), jnp.float32), 'spatial_encoding': jax.random.normal(ks[1], (B, N, N), jnp.float32), 'edge_encoding': jax.random.normal(ks[2], (B, N, N), jnp.float32), 'Wq': jax.random.normal(ks[3], (HIDDEN, HIDDEN), jnp.float32) * s, 'Wk': jax.random.normal(ks[4], (HIDDEN, HIDDEN), jnp.float32) * s, 'Wv': jax.random.normal(ks[5], (HIDDEN, HIDDEN), jnp.float32) * s, 'bv': jax.random.normal(ks[6], (HIDDEN,), jnp.float32) * s, 'Wo': jax.random.normal(ks[7], (HIDDEN, HIDDEN), jnp.float32) * s, 'bo': jax.random.normal(ks[8], (HIDDEN,), jnp.float32) * s}
    _L0_gnn_all = _L0_gnn_setup()
    _L0_gnn_in = {k: v for k, v in _L0_gnn_all.items() if k in ('Wq', 'Wk', 'Wv', 'bv', 'Wo', 'bo')}
    del _L0_gnn_all

    def _L1_gnn_setup():
        import jax, jax.numpy as jnp
        import numpy as np
        B, N, D, H = (8, 512, 384, 12)
        HD = D // H

        def _split_heads(x):
            b, n, _ = x.shape
            return x.reshape(b, n, H, HD).transpose(0, 2, 1, 3)
        key = jax.random.key(seed)
        ks = jax.random.split(key, 10)
        input_graph = jax.random.normal(ks[0], (B, N, D), dtype=jnp.float32)
        u = jax.random.uniform(ks[1], (B, N, N), dtype=jnp.float32)
        keep = jax.random.uniform(ks[2], (B, N, N)) < 0.15
        adj = jnp.where(keep, u, 0.0)
        s = 1.0 / np.sqrt(D)
        Wq = jax.random.normal(ks[3], (D, D), dtype=jnp.float32) * s
        bq = jnp.zeros((D,), dtype=jnp.float32)
        Wk = jax.random.normal(ks[4], (D, D), dtype=jnp.float32) * s
        bk = jnp.zeros((D,), dtype=jnp.float32)
        Wv = jax.random.normal(ks[5], (D, D), dtype=jnp.float32) * s
        bv = jnp.zeros((D,), dtype=jnp.float32)
        beta = jnp.asarray(0.1, dtype=jnp.float32)
        return {'input_graph': input_graph, 'adj': adj, 'Wq': Wq, 'bq': bq, 'Wk': Wk, 'bk': bk, 'Wv': Wv, 'bv': bv, 'beta': beta}
    _L1_gnn_all = _L1_gnn_setup()
    _L1_gnn_in = {k: v for k, v in _L1_gnn_all.items() if k in ('Wq', 'bq', 'Wk', 'bk', 'Wv', 'bv', 'beta')}
    del _L1_gnn_all
    return {'x': x, 'adj': adj, 'L0_gnn_Wq': _L0_gnn_in['Wq'], 'L0_gnn_Wk': _L0_gnn_in['Wk'], 'L0_gnn_Wv': _L0_gnn_in['Wv'], 'L0_gnn_bv': _L0_gnn_in['bv'], 'L0_gnn_Wo': _L0_gnn_in['Wo'], 'L0_gnn_bo': _L0_gnn_in['bo'], 'L1_gnn_Wq': _L1_gnn_in['Wq'], 'L1_gnn_bq': _L1_gnn_in['bq'], 'L1_gnn_Wk': _L1_gnn_in['Wk'], 'L1_gnn_bk': _L1_gnn_in['bk'], 'L1_gnn_Wv': _L1_gnn_in['Wv'], 'L1_gnn_bv': _L1_gnn_in['bv'], 'L1_gnn_beta': _L1_gnn_in['beta']}

def reference(x, adj, L0_gnn_Wq, L0_gnn_Wk, L0_gnn_Wv, L0_gnn_bv, L0_gnn_Wo, L0_gnn_bo, L1_gnn_Wq, L1_gnn_bq, L1_gnn_Wk, L1_gnn_bk, L1_gnn_Wv, L1_gnn_bv, L1_gnn_beta):
    import jax
    import jax.numpy as jnp

    def _L0_gnn_ref(x, spatial_encoding, edge_encoding, Wq, Wk, Wv, bv, Wo, bo):
        import jax, jax.numpy as jnp
        import numpy as np
        NUM_HEADS = 12
        HIDDEN = 384
        HEAD = HIDDEN // NUM_HEADS
        B, N = (16, 256)
        b, n, h = x.shape
        scale = jnp.asarray(HIDDEN, x.dtype) ** (-0.5)
        q = (x @ Wq.T).reshape(b, n, NUM_HEADS, HEAD)
        k = (x @ Wk.T).reshape(b, n, NUM_HEADS, HEAD)
        v = (x @ Wv.T + bv).reshape(b, n, NUM_HEADS, HEAD)
        bias = (spatial_encoding + edge_encoding)[:, None]
        scores = jnp.einsum('bqhd,bkhd->bhqk', q, k) * scale + bias
        row_nonzero = jnp.any(scores != 0, axis=-1, keepdims=True)
        scores = jnp.where(row_nonzero, scores, -jnp.inf)
        p = jax.nn.softmax(scores, axis=-1)
        p = jnp.nan_to_num(p)
        out = jnp.einsum('bhqk,bkhd->bqhd', p, v).reshape(b, n, h)
        return out @ Wo.T + bo

    def _L1_gnn_ref(input_graph, adj, Wq, bq, Wk, bk, Wv, bv, beta):
        import jax, jax.numpy as jnp
        import numpy as np
        B, N, D, H = (8, 512, 384, 12)
        HD = D // H

        def _split_heads(x):
            b, n, _ = x.shape
            return x.reshape(b, n, H, HD).transpose(0, 2, 1, 3)
        q = _split_heads(input_graph @ Wq + bq)
        k = _split_heads(input_graph @ Wk + bk)
        v = _split_heads(input_graph @ Wv + bv)
        scores = jnp.einsum('bhqd,bhkd->bhqk', q, k) / jnp.sqrt(jnp.asarray(HD, input_graph.dtype))
        adj_e = adj[:, None, :, :]
        scores = scores + beta * adj_e
        scores = jnp.where(adj_e > 0, scores, jnp.asarray(-9000000000000000.0, scores.dtype))
        probs = jax.nn.softmax(scores, axis=-1)
        out = jnp.einsum('bhqk,bhkd->bhqd', probs, v)
        return out.transpose(0, 2, 1, 3).reshape(input_graph.shape[0], input_graph.shape[1], D)
    x = _layernorm(x + _L0_gnn_ref(x, adj, adj, L0_gnn_Wq, L0_gnn_Wk, L0_gnn_Wv, L0_gnn_bv, L0_gnn_Wo, L0_gnn_bo), axis=-1)
    x = _layernorm(x + _L1_gnn_ref(x, adj, L1_gnn_Wq, L1_gnn_bq, L1_gnn_Wk, L1_gnn_bk, L1_gnn_Wv, L1_gnn_bv, L1_gnn_beta), axis=-1)
    return x

_drawn_inputs = setup_inputs


def setup_inputs(seed=0):
    import zlib

    import numpy as np

    out = dict(_drawn_inputs(seed))
    spreads = {'L1_gnn_bq': (0.0, 0.1), 'L1_gnn_bk': (0.0, 0.8), 'L1_gnn_bv': (0.0, 0.1)}
    factors = {'L0_gnn_Wq': 8.0, 'L0_gnn_Wk': 8.0, 'L0_gnn_bv': 4.871}
    for name, (base, spread) in spreads.items():
        noise = np.random.default_rng([zlib.crc32(name.encode()), seed]).standard_normal(out[name].shape)
        drawn = base * np.exp(spread * noise) if base else spread * noise
        out[name] = jnp.asarray(drawn.astype(out[name].dtype))
    for name, factor in factors.items():
        out[name] = (out[name] * factor).astype(out[name].dtype)
    return out
```

```python
from contextlib import ExitStack

import concourse.bass as bass
from concourse import mybir

F32 = mybir.dt.float32
F32R = mybir.dt.float32r
ALU = mybir.AluOpType
ACT = mybir.ActivationFunctionType
AX_X = mybir.AxisListType.X

NG, N, D = 128, 128, 384
H, HD = 12, 32
P = 128
C = D // P
HC = H // C
PAIRS = NG // 2
G2 = 2 * N
EPS = 1e-5
MASKED = 9000000000000000.0
SCALE0 = float(D) ** -0.5
SCALE1 = float(HD) ** -0.5
BIG = 3.0e38

FIRST, LAST = -1, PAIRS + 2
LOOP_FROM = 3
LOOP_N = PAIRS - 3 - LOOP_FROM
assert LOOP_N % 2 == 0

BANK_HEADS = [[b, b + HC, b + 2 * HC] for b in range(HC)]

RING = (["xt0", "xt1", "x1t0", "x1t1", "pv1_0", "g0_0", "g0_1", "g0_2", "ot_0", "v0_0", "g1_0",
         "pv0_0", "g1_1", "g1_2", "v1_0", "wo_0"]
        + ["g0_3", "pv1_1", "g0_4", "g0_5", "ot_1", "v0_1", "g1_3", "pv0_1", "g1_4", "g1_5",
           "v1_1", "wo_1"])
assert len(RING) % 2 == 0
RING_BANK = {name: i % 2 for i, name in enumerate(RING)}


class Pair:

    def __init__(self, r, off):
        self.r, self.off = r, off
        self.parity = off % 2

    def plus(self, d):
        return Pair(self.r, self.off + d)

    def index(self):
        return self.r + self.off

    def count(self, per_graph, g, plus):
        value = 2 * per_graph * self.r + (per_graph * (2 * self.off + g) + plus)
        return max(value, 0) if isinstance(value, int) else value

    def loads(self):
        return 8 * self.r + 16 * (self.off // 2 + 1)

    def valid(self):
        return not isinstance(self.r, int) or 0 <= self.r + self.off < PAIRS


def iterations(eng, body, after_loop=None):
    for n in range(FIRST, LOOP_FROM):
        body(0, n)
    with eng.Fori(0, LOOP_N // 2) as turn:
        for u in range(2):
            body(2 * turn, LOOP_FROM + u)
    if after_loop:
        after_loop()
    for n in range(LOOP_FROM + LOOP_N, LAST + 1):
        body(LOOP_N, n - LOOP_N)


def build(nc, x, adj, wts, bv0, bo0, bq1, bk1, bv1, beta, out):
    with ExitStack() as ctx:
        def sb(name, shape, dt=F32):
            return ctx.enter_context(nc.sbuf_tensor(name, shape, dt))

        def bank(name):
            return ctx.enter_context(nc.psum_tensor(name, [P, 512], F32))

        def sem(name):
            return ctx.enter_context(nc.semaphore(name))

        def sems(name, n=2):
            return [sem(f"{name}_{i}") for i in range(n)]

        NW = 7
        WQ0, WK0, WV0, WO0, WQ1, WK1, WV1 = range(NW)
        w_stage = [sb(f"w_stage{i}", [P, C, D]) for i in range(2)]
        w_hi = [sb(f"w_hi{i}", [P, C, D], F32R) for i in range(NW)]
        w_lo = [sb(f"w_lo{i}", [P, C, D], F32R) for i in range(NW)]
        ident = sb("ident", [P, P])
        bv_row = [sb("bv0_row", [P, D]), sb("bv1_row", [P, D])]
        bo_row = sb("bo_row", [P, D])
        bqk1 = sb("bqk1", [P, 2, C])
        bq1s = sb("bq1s", [P, C])
        beta_col = sb("beta_col", [P, 1])
        neg_half = sb("neg_half", [P, 1])
        x_in = [sb(f"x_in{b}", [P, 2, D]) for b in range(2)]
        x_bo = [sb(f"x_bo{b}", [P, 2, D]) for b in range(2)]
        adj0 = [sb(f"adj0_{b}", [P, 2, N]) for b in range(2)]
        adj1 = [sb(f"adj1_{b}", [P, 2, N]) for b in range(2)]
        bias = [[sb(f"bias{l}_{b}", [P, 2, N]) for b in range(2)] for l in range(2)]
        qT = [[sb(f"q{l}T_{b}", [P, C, G2]) for b in range(2)] for l in range(2)]
        kT = [[sb(f"k{l}T_{b}", [P, C, G2]) for b in range(2)] for l in range(2)]
        v = [[sb(f"v{l}_{b}", [P, 2, D]) for b in range(2)] for l in range(2)]
        x1 = [sb(f"x1_{b}", [P, 2, D]) for b in range(2)]
        x1_late = [sb(f"x1_late{b}", [P, 2, D]) for b in range(2)]
        xT_hi, xT_lo = sb("xT_hi", [P, C, G2], F32R), sb("xT_lo", [P, C, G2], F32R)
        x1T_hi, x1T_lo = sb("x1T_hi", [P, C, G2], F32R), sb("x1T_lo", [P, C, G2], F32R)
        neg_s = [sb(f"neg_s{l}", [P, H, N]) for l in range(2)]
        neg_max = [sb(f"neg_max{l}", [P, H]) for l in range(2)]
        prob = [sb(f"prob{l}", [P, H, N]) for l in range(2)]
        row_sum = [sb(f"row_sum{l}", [P, H]) for l in range(2)]
        inv_sum = [sb(f"inv_sum{l}", [P, H]) for l in range(2)]
        inv_raw0 = sb("inv_raw0", [P, H])
        abs_max0 = sb("abs_max0", [P, H])
        probT = [[sb(f"prob{l}T_{c}", [P, HC, N]) for c in range(C)] for l in range(2)]
        o0T_hi, o0T_lo = sb("o0T_hi", [P, C, N], F32R), sb("o0T_lo", [P, C, N], F32R)
        o1T = sb("o1T", [P, C, N])
        y = [sb(f"y{l}", [P, D]) for l in range(2)]
        stats = [sb(f"stats{l}", [P, 6]) for l in range(2)]
        mean_var = [sb(f"mean_var{l}", [P, 2]) for l in range(2)]
        var_eps = [sb(f"var_eps{l}", [P, 1]) for l in range(2)]
        rstd = [sb(f"rstd{l}", [P, 1]) for l in range(2)]
        mask1, linear1 = sb("mask1", [P, 2, N]), sb("linear1", [P, 2, N])
        x2 = [sb(f"x2_{g}", [P, D]) for g in range(2)]

        s_bank = [bank(f"s_bank{i}") for i in range(HC)]
        a_bank = [bank(f"a_bank{i}") for i in range(2)]
        t_bank = [bank(f"t_bank{i}") for i in range(2)]

        def ring(name):
            return a_bank[RING_BANK[name]]

        def t_index(layer, g, c):
            return (2 * C * g + (0 if layer else C) + c) % 2

        w_loaded = sems("w_loaded")
        small_loaded = sem("small_loaded")
        x_loaded, adj0_loaded, adj1_loaded = sems("x_loaded"), sems("adj0_loaded"), sems("adj1_loaded")
        stored = sems("stored")
        w_hi_done, w_lo_done = sem("w_hi_done"), sem("w_lo_done")
        const_done = sem("const_done")
        ident_done = sem("ident_done")
        dve_passed, pool_passed = sem("dve_passed"), sem("pool_passed")
        xt_done, x1t_done = sem("xt_done"), sem("x1t_done")
        g_done = sems("g_done")
        v_done = sems("v_done")
        s_done = sems("s_done")
        pt_done = sems("pt_done")
        pv_done = sems("pv_done")
        wo_done, ot_done = sem("wo_done"), sem("ot_done")
        xt_hi_done, x1t_hi_done, o0t_hi_done = sem("xt_hi_done"), sem("x1t_hi_done"), sem("o0t_hi_done")
        g_out = sems("g_out")
        exp_done = sems("exp_done")
        xt_lo_done, x1t_lo_done, o0t_lo_done = sem("xt_lo_done"), sem("x1t_lo_done"), sem("o0t_lo_done")
        v_out = sems("v_out")
        o1t_out = sem("o1t_out")
        neg_done = sems("neg_done")
        absmax_done = sem("absmax_done")
        inv0_steps = sem("inv0_steps")
        inv1_done = sem("inv1_done")
        y0_done, y1_att_done = sem("y0_done"), sem("y1_att_done")
        norm_stats = sems("norm_stats")
        x1_done, x2_done = sem("x1_done"), sem("x2_done")
        x_bo_done, bias0_done, bias1_steps = sem("x_bo_done"), sem("bias0_done"), sem("bias1_steps")
        x1_late_done = sem("x1_late_done")
        rstd_steps = sems("rstd_steps")
        probn_done = sem("probn_done")
        y1_done = sem("y1_done")
        pt_out = [sems(f"pt{l}_out", C) for l in range(2)]

        block = ctx.enter_context(nc.Block())

        @block.sync
        def _(sp):
            def load_x(q):
                if q.valid():
                    b = q.parity
                    sp.wait_ge(xt_done, q.plus(-2).count(1, 1, 1))
                    sp.wait_ge(x_bo_done, q.plus(-2).count(1, 1, 1))
                    sp.dma_start(x_in[b][:], x[bass.ds(2 * q.index(), 2)].rearrange("g n d -> n g d")
                                 ).then_inc(x_loaded[b], 16)
                    sp.wait_ge(bias0_done, q.plus(-2).count(1, 1, 1))
                    sp.dma_start(adj0[b][:], adj[bass.ds(2 * q.index(), 2)].rearrange("g n k -> n g k")
                                 ).then_inc(adj0_loaded[b], 16)

            def load_adj1(q):
                if q.valid():
                    b = q.parity
                    sp.wait_ge(bias1_steps, q.plus(-2).count(5, 1, 5))
                    sp.dma_start(adj1[b][:], adj[bass.ds(2 * q.index(), 2)].rearrange("g n k -> n g k")
                                 ).then_inc(adj1_loaded[b], 16)

            def store(q, g):
                if q.valid():
                    sp.wait_ge(x2_done, q.count(1, g, 1))
                    sp.dma_start(out[bass.ds(2 * q.index() + g, 1)].rearrange("g n d -> n (g d)"), x2[g][:]
                                 ).then_inc(stored[g], 16)

            load_x(Pair(0, 0))
            for i in range(NW):
                sp.wait_ge(w_lo_done, max(i - 1, 0))
                sp.dma_start(w_stage[i % 2][:], wts[i].rearrange("(c p) o -> p c o", p=P)
                             ).then_inc(w_loaded[i % 2], 16)
                if i == 1:
                    sp.dma_start(bv_row[0][:], bv0.partition_broadcast(P)).then_inc(small_loaded, 16)
                    sp.dma_start(bv_row[1][:], bv1.partition_broadcast(P)).then_inc(small_loaded, 16)
                    sp.dma_start(bo_row[:], bo0.partition_broadcast(P)).then_inc(small_loaded, 16)
                    sp.dma_start(beta_col[:], beta.partition_broadcast(P)).then_inc(small_loaded, 16)
                    for j, b_ in enumerate((bq1, bk1)):
                        sp.dma_start(bqk1[:, j, :], b_.rearrange("(c p) -> p c", p=P),
                                     allow_slow_non_contiguous=True).then_inc(small_loaded, 16)
            load_x(Pair(0, 1))

            def body(r, off):
                n = Pair(r, off)
                load_x(n.plus(3))
                store(n.plus(-3), 1)
                load_adj1(n.plus(1))
                store(n.plus(-2), 0)

            iterations(sp, body)
            for g in range(2):
                sp.wait_ge(stored[g], 16 * PAIRS)

        @block.tensor
        def _(pe):
            a_read = [(xt_lo_done, 0, 0, 0, 0)] * 2
            s_read = [(neg_done[0], 0, 0, 0, 0)] * HC
            t_read = [(exp_done[1], 0, 0, 0, 0)] * 2

            def last_read(table, i, r):
                sem_, off, per, g, plus = table[i]
                return sem_, Pair(r, off).count(per, g, plus)

            def after_loop():
                for table in (a_read, s_read, t_read):
                    for i, (sem_, off, per, g, plus) in enumerate(table):
                        table[i] = (sem_, off - 2, per, g, plus)

            def transpose_x(q, g, r):
                if q.valid():
                    pe.wait_ge(*last_read(a_read, RING_BANK[f"xt{g}"], r))
                    a_read[RING_BANK[f"xt{g}"]] = (xt_lo_done, q.off, 1, g, 1)
                    pe.wait_ge(x_loaded[q.parity], q.loads())
                    for c in range(C):
                        mm = pe.transpose(ring(f"xt{g}")[:, c * P:(c + 1) * P],
                                          x_in[q.parity][:, g, c * P:(c + 1) * P], ident[:])
                    mm.then_inc(xt_done, 1)

            def transpose_x1(q, g, r):
                if q.valid():
                    pe.wait_ge(*last_read(a_read, RING_BANK[f"x1t{g}"], r))
                    a_read[RING_BANK[f"x1t{g}"]] = (x1t_lo_done, q.off, 1, g, 1)
                    pe.wait_ge(x1_done, q.count(1, g, 1))
                    for c in range(C):
                        mm = pe.transpose(ring(f"x1t{g}")[:, c * P:(c + 1) * P],
                                          x1[q.parity][:, g, c * P:(c + 1) * P], ident[:])
                    mm.then_inc(x1t_done, 1)

            def split_product(dst, a_hi, a_lo, b_hi, b_lo):
                for c in range(C):
                    pe.matmul(dst, a_hi(c), b_hi(c), start=(c == 0), stop=False)
                    pe.matmul(dst, a_hi(c), b_lo(c), start=False, stop=False)
                    mm = pe.matmul(dst, a_lo(c), b_hi(c), start=False, stop=(c == C - 1))
                return mm

            t_hi, t_lo = (xT_hi, x1T_hi), (xT_lo, x1T_lo)
            lo_done = (xt_lo_done, x1t_lo_done)

            def project_qk(layer, q, j, r):
                if q.valid():
                    name = f"g{layer}_{j}"
                    pe.wait_ge(*last_read(a_read, RING_BANK[name], r))
                    a_read[RING_BANK[name]] = (g_out[layer], q.off, 3, 0, j + 1)
                    pe.wait_ge(lo_done[layer], q.count(1, 1, 1))
                    wi = ((WQ0, WK0), (WQ1, WK1))[layer][j // C]
                    if q.off == 0 and isinstance(r, int) and r == 0:
                        pe.wait_ge(w_lo_done, wi + 1)
                    f = slice((j % C) * P, (j % C + 1) * P)
                    split_product(ring(name)[:, 0:G2], lambda c: w_hi[wi][:, c, f], lambda c: w_lo[wi][:, c, f],
                                  lambda c: t_hi[layer][:, c, :], lambda c: t_lo[layer][:, c, :]
                                  ).then_inc(g_done[layer], 1)

            def project_v(layer, q, g, r):
                if q.valid():
                    name = f"v{layer}_{g}"
                    pe.wait_ge(*last_read(a_read, RING_BANK[name], r))
                    a_read[RING_BANK[name]] = (v_out[layer], q.off, 1, g, 1)
                    wi = (WV0, WV1)[layer]
                    if q.off == 0 and isinstance(r, int) and r == 0:
                        pe.wait_ge(w_lo_done, wi + 1)
                    m = slice(g * N, (g + 1) * N)
                    split_product(ring(name)[:, 0:D], lambda c: t_hi[layer][:, c, m], lambda c: t_lo[layer][:, c, m],
                                  lambda c: w_hi[wi][:, c, :], lambda c: w_lo[wi][:, c, :]
                                  ).then_inc(v_done[layer], 1)

            def scores(layer, q, g, r):
                if q.valid():
                    pe.wait_ge(g_out[layer], q.count(3, 1, 3))
                    m = slice(g * N, (g + 1) * N)
                    for h in range(H):
                        c, j = divmod(h, HC)
                        if c == 0:
                            pe.wait_ge(*last_read(s_read, j, r))
                            s_read[j] = (neg_done[layer], q.off, H, g, C * (j + 1))
                        rows = slice(HD * j, HD * (j + 1))
                        mm = pe.matmul(s_bank[j][:, c * N:(c + 1) * N], qT[layer][q.parity][rows, c, m],
                                       kT[layer][q.parity][rows, c, m], start=True, stop=True)
                        if c == C - 1:
                            mm.then_inc(s_done[layer], 1)

            def transpose_probs(layer, q, g, c, r):
                if q.valid():
                    i = t_index(layer, g, c)
                    pe.wait_ge(*last_read(t_read, i, r))
                    t_read[i] = (pt_out[layer][c], q.off, 1, g, 1)
                    if layer == 0:
                        pe.wait_ge(probn_done, q.count(C, g, c + 1))
                    else:
                        pe.wait_ge(exp_done[1], q.count(H, g, H))
                    for j in range(HC):
                        mm = pe.transpose(t_bank[i][:, j * N:(j + 1) * N], prob[layer][:, HC * c + j, :], ident[:])
                    mm.then_inc(pt_done[layer], 1)

            def attend(layer, q, g, c, r):
                if q.valid():
                    name = f"pv{layer}_{g}"
                    if c == 0:
                        pe.wait_ge(*last_read(a_read, RING_BANK[name], r))
                        a_read[RING_BANK[name]] = ((o0t_lo_done, o1t_out)[layer], q.off, 1, g, 1)
                        pe.wait_ge(v_out[layer], q.count(1, g, 1))
                    pe.wait_ge(pt_out[layer][c], q.count(1, g, 1))
                    for j in range(HC):
                        f = slice(HD * (HC * c + j), HD * (HC * c + j + 1))
                        mm = pe.matmul(ring(name)[HD * j:HD * (j + 1), c * N:(c + 1) * N],
                                       v[layer][q.parity][:, g, f], probT[layer][c][:, j, :],
                                       start=True, stop=True)
                    mm.then_inc(pv_done[layer], 1)

            def transpose_out1(q, g, r):
                if q.valid():
                    name = f"ot_{g}"
                    pe.wait_ge(*last_read(a_read, RING_BANK[name], r))
                    a_read[RING_BANK[name]] = (y1_att_done, q.off, 1, g, 1)
                    pe.wait_ge(o1t_out, q.count(1, g, 1))
                    for c in range(C):
                        mm = pe.transpose(ring(name)[:, c * P:(c + 1) * P], o1T[:, c, :], ident[:])
                    mm.then_inc(ot_done, 1)

            def project_out0(q, g, r):
                if q.valid():
                    name = f"wo_{g}"
                    pe.wait_ge(*last_read(a_read, RING_BANK[name], r))
                    a_read[RING_BANK[name]] = (y0_done, q.off, 1, g, 1)
                    pe.wait_ge(o0t_lo_done, q.count(1, g, 1))
                    if q.off == 0 and isinstance(r, int) and r == 0:
                        pe.wait_ge(w_lo_done, WO0 + 1)
                    split_product(ring(name)[:, 0:D], lambda c: o0T_hi[:, c, :], lambda c: o0T_lo[:, c, :],
                                  lambda c: w_hi[WO0][:, c, :], lambda c: w_lo[WO0][:, c, :]
                                  ).then_inc(wo_done, 1)

            pe.wait_ge(ident_done, 2)

            def body(r, off):
                n = Pair(r, off)
                nxt, prev, prev2 = n.plus(1), n.plus(-1), n.plus(-2)
                for s in range(2):
                    late, lg = (n.plus(-3), 1) if s == 0 else (prev2, 0)
                    scores(0, n, s, r)
                    if s == 0:
                        transpose_x(nxt, 0, r)
                        transpose_x(nxt, 1, r)
                    transpose_probs(1, late, lg, 0, r)
                    transpose_probs(1, late, lg, 1, r)
                    if s == 0:
                        transpose_x1(prev, 0, r)
                        transpose_x1(prev, 1, r)
                    else:
                        project_qk(0, nxt, 3, r)
                    transpose_probs(1, late, lg, 2, r)
                    for c in range(C):
                        attend(1, late, lg, c, r)
                    for j in (0, 1, 2) if s == 0 else (4, 5):
                        project_qk(0, nxt, j, r)
                    transpose_out1(late, lg, r)
                    project_v(0, nxt, s, r)
                    scores(1, prev2, s, r)
                    transpose_probs(0, n, s, 0, r)
                    transpose_probs(0, n, s, 1, r)
                    project_qk(1, prev, 3 * s, r)
                    transpose_probs(0, n, s, 2, r)
                    for c in range(C):
                        attend(0, n, s, c, r)
                    project_qk(1, prev, 3 * s + 1, r)
                    project_qk(1, prev, 3 * s + 2, r)
                    project_v(1, prev, s, r)
                    project_out0(n, s, r)

            iterations(pe, body, after_loop)

        @block.scalar
        def _(act):
            for i in range(NW):
                act.wait_ge(w_loaded[i % 2], 16 * (i // 2 + 1))
                act.activation(w_hi[i][:], w_stage[i % 2][:], ACT.Copy).then_inc(w_hi_done, 1)

            def high_xT(q, g):
                if q.valid():
                    act.wait_ge(xt_done, q.count(1, g, 1))
                    if g == 0:
                        act.wait_ge(v_done[0], q.count(1, 0, 0))
                    act.activation(xT_hi[:, :, g * N:(g + 1) * N],
                                   ring(f"xt{g}")[:, 0:D].rearrange("p (c n) -> p c n", c=C), ACT.Copy
                                   ).then_inc(xt_hi_done, 1)

            def high_x1T(q, g):
                if q.valid():
                    act.wait_ge(x1t_done, q.count(1, g, 1))
                    if g == 0:
                        act.wait_ge(v_done[1], q.count(1, 0, 0))
                    act.activation(x1T_hi[:, :, g * N:(g + 1) * N],
                                   ring(f"x1t{g}")[:, 0:D].rearrange("p (c n) -> p c n", c=C), ACT.Copy
                                   ).then_inc(x1t_hi_done, 1)

            def high_o0T(q, g):
                if q.valid():
                    act.wait_ge(pv_done[0], q.count(C, g, C))
                    act.wait_ge(wo_done, q.count(1, g, 0))
                    act.activation(o0T_hi[:], ring(f"pv0_{g}")[:, 0:D].rearrange("p (c n) -> p c n", c=C),
                                   ACT.Copy).then_inc(o0t_hi_done, 1)

            def qk_out(layer, q, j):
                if q.valid():
                    b, c = q.parity, j % C
                    act.wait_ge(g_done[layer], q.count(3, 0, j + 1))
                    act.wait_ge(s_done[layer], q.plus(-2).count(HC, 1, HC))
                    src = ring(f"g{layer}_{j}")[:, 0:G2]
                    if layer == 0:
                        dst = (qT if j < C else kT)[0][b][:, c, :]
                        ins = act.activation(dst, src, ACT.Copy, scale=SCALE0 if j < C else 1.0)
                    elif j < C:
                        ins = act.activation(qT[1][b][:, c, :], src, ACT.Identity, bias=bq1s[:, c:c + 1], scale=SCALE1)
                    else:
                        ins = act.activation(kT[1][b][:, c, :], src, ACT.Identity, bias=bqk1[:, 1, c:c + 1])
                    ins.then_inc(g_out[layer], 1)

            def probT_out(layer, q, g, c):
                if q.valid():
                    act.wait_ge(pt_done[layer], q.count(C, g, c + 1))
                    act.wait_ge(pv_done[layer], q.count(C, g, c + 1 - C))
                    act.activation(probT[layer][c][:],
                                   t_bank[t_index(layer, g, c)][:].rearrange("p (j n) -> p j n", j=HC), ACT.Copy
                                   ).then_inc(pt_out[layer][c], 1)

            def exps(layer, q, g, b):
                if q.valid():
                    if b == 0:
                        act.wait_ge(pt_done[layer], q.count(C, g, 0))
                        if layer == 1:
                            act.wait_ge(inv1_done, q.count(1, g, 0))
                    for i, h in enumerate(BANK_HEADS[b]):
                        act.wait_ge(neg_done[layer], q.count(H, g, C * b + i + 1))
                        act.activation(prob[layer][:, h, :], neg_s[layer][:, h, :], ACT.Exp,
                                       bias=neg_max[layer][:, h:h + 1], scale=-1.0,
                                       accum_out=row_sum[layer][:, h:h + 1]).then_inc(exp_done[layer], 1)

            act.wait_ge(const_done, 2)
            act.wait_ge(small_loaded, 16 * 6)

            def body(r, off):
                n = Pair(r, off)
                nxt, prev, prev2 = n.plus(1), n.plus(-1), n.plus(-2)
                for s in range(2):
                    late, lg = (n.plus(-3), 1) if s == 0 else (prev2, 0)
                    if s == 0:
                        high_xT(nxt, 0)
                        high_xT(nxt, 1)
                        probT_out(1, late, lg, 0)
                        high_x1T(prev, 0)
                        high_x1T(prev, 1)
                        probT_out(1, late, lg, 2)
                        exps(0, n, s, 0)
                        qk_out(0, nxt, 0)
                        exps(0, n, s, 1)
                        qk_out(0, nxt, 1)
                        exps(0, n, s, 2)
                        qk_out(0, nxt, 2)
                        exps(0, n, s, 3)
                    else:
                        probT_out(1, late, lg, 0)
                        exps(0, n, s, 0)
                        qk_out(0, nxt, 3)
                        probT_out(1, late, lg, 2)
                        exps(0, n, s, 1)
                        qk_out(0, nxt, 4)
                        exps(0, n, s, 2)
                        qk_out(0, nxt, 5)
                        exps(0, n, s, 3)
                    probT_out(0, n, s, 0)
                    exps(1, prev2, s, 0)
                    qk_out(1, prev, 3 * s)
                    probT_out(0, n, s, 2)
                    exps(1, prev2, s, 1)
                    high_o0T(n, s)
                    exps(1, prev2, s, 2)
                    qk_out(1, prev, 3 * s + 1)
                    qk_out(1, prev, 3 * s + 2)
                    exps(1, prev2, s, 3)

            iterations(act, body)

        @block.vector
        def _(dve):
            for i in range(NW):
                dve.wait_ge(w_hi_done, i + 1)
                dve.tensor_tensor(w_lo[i][:], w_stage[i % 2][:], w_hi[i][:].bitcast(F32), ALU.subtract
                                  ).then_inc(w_lo_done, 1)
            dve.wait_ge(small_loaded, 16 * 6)

            def norm_input0(q, g):
                if q.valid():
                    dve.wait_ge(wo_done, q.count(1, g, 1))
                    dve.wait_ge(x_bo_done, q.count(1, 1, 1))
                    dve.wait_ge(x1_done, q.count(1, g, 0))
                    dve.tensor_tensor(y[0][:], ring(f"wo_{g}")[:, 0:D], x_bo[q.parity][:, g, :], ALU.add
                                      ).then_inc(y0_done, 1)
                    dve.wait_ge(y0_done, q.count(1, g, 1))
                    norm_stats_of(0, q, g)

            def norm_stats_of(layer, q, g):
                dve.bn_stats(stats[layer][:], y[layer][:]).then_inc(norm_stats[layer], 1)
                dve.wait_ge(norm_stats[layer], q.count(2, g, 1))
                dve.sem_inc(dve_passed, 1)
                dve.bn_aggr(mean_var[layer][:], stats[layer][:]).then_inc(norm_stats[layer], 1)

            def norm_apply0(q, g):
                if q.valid():
                    dve.wait_ge(rstd_steps[0], q.count(2, g, 2))
                    dve.wait_ge(x1t_done, q.plus(-2).count(1, g, 1))
                    dve.wait_ge(x1_late_done, q.plus(-2).count(1, 1, 1))
                    dve.tensor_scalar(x1[q.parity][:, g, :], y[0][:], mean_var[0][:, 0:1], rstd[0][:],
                                      ALU.subtract, ALU.mult).then_inc(x1_done, 1)

            def negate(layer, q, g, banks):
                if q.valid():
                    for b in banks:
                        if b == 0:
                            if layer == 0:
                                dve.wait_ge(bias0_done, q.count(1, 1, 1))
                                dve.wait_ge(absmax_done, q.count(1, g, 0))
                            else:
                                dve.wait_ge(bias1_steps, q.count(5, 1, 5))
                            dve.wait_ge(exp_done[layer], q.count(H, g, 0))
                        dve.wait_ge(s_done[layer], q.count(HC, g, b + 1))
                        dve.sem_inc(dve_passed, 1)
                        for h in BANK_HEADS[b]:
                            dve.tensor_tensor_reduce(neg_s[layer][:, h, :],
                                                     s_bank[b][:, (h // HC) * N:(h // HC + 1) * N],
                                                     bias[layer][q.parity][:, g, :], -1.0, BIG, ALU.add, ALU.min,
                                                     neg_max[layer][:, h:h + 1]).then_inc(neg_done[layer], 1)

            def probT_out(layer, q, g):
                if q.valid():
                    dve.wait_ge(pt_done[layer], q.count(C, g, 2))
                    dve.wait_ge(pv_done[layer], q.count(C, g, 2 - C))
                    dve.tensor_copy(probT[layer][1][:],
                                    t_bank[t_index(layer, g, 1)][:].rearrange("p (j n) -> p j n", j=HC)
                                    ).then_inc(pt_out[layer][1], 1)

            def low_part(dst, name, hi, hi_done, done, q, g):
                dve.wait_ge(hi_done, q.count(1, g, 1))
                dve.tensor_tensor(dst, ring(name)[:, 0:D].rearrange("p (c n) -> p c n", c=C), hi.bitcast(F32),
                                  ALU.subtract).then_inc(done, 1)

            def low_xT(q, g):
                if q.valid():
                    if g == 0:
                        dve.wait_ge(v_done[0], q.count(1, 0, 0))
                    m = slice(g * N, (g + 1) * N)
                    low_part(xT_lo[:, :, m], f"xt{g}", xT_hi[:, :, m], xt_hi_done, xt_lo_done, q, g)

            def low_x1T(q, g):
                if q.valid():
                    if g == 0:
                        dve.wait_ge(v_done[1], q.count(1, 0, 0))
                    m = slice(g * N, (g + 1) * N)
                    low_part(x1T_lo[:, :, m], f"x1t{g}", x1T_hi[:, :, m], x1t_hi_done, x1t_lo_done, q, g)

            def low_o0T(q, g):
                if q.valid():
                    dve.wait_ge(wo_done, q.count(1, g, 0))
                    low_part(o0T_lo[:], f"pv0_{g}", o0T_hi[:], o0t_hi_done, o0t_lo_done, q, g)

            def out1T_out(q, g):
                if q.valid():
                    dve.wait_ge(pv_done[1], q.count(C, g, C))
                    dve.wait_ge(ot_done, q.count(1, g, 0))
                    dve.tensor_copy(o1T[:], ring(f"pv1_{g}")[:, 0:D].rearrange("p (c n) -> p c n", c=C)
                                    ).then_inc(o1t_out, 1)

            def abs_max(q, g):
                if q.valid():
                    dve.wait_ge(neg_done[0], q.count(H, g, H))
                    dve.wait_ge(inv0_steps, q.count(2, g, 0))
                    dve.tensor_reduce(abs_max0[:], neg_s[0][:], AX_X, ALU.max, apply_absolute_value=True
                                      ).then_inc(absmax_done, 1)

            def inverse_sums1(q, g):
                if q.valid():
                    dve.wait_ge(exp_done[1], q.count(H, g, H))
                    dve.wait_ge(y1_att_done, q.count(1, g, 0))
                    dve.reciprocal(inv_sum[1][:], row_sum[1][:]).then_inc(inv1_done, 1)

            def attention_out1(q, g):
                if q.valid():
                    dve.wait_ge(ot_done, q.count(1, g, 1))
                    dve.wait_ge(inv1_done, q.count(1, g, 1))
                    dve.wait_ge(x2_done, q.count(1, g, 0))
                    dve.tensor_tensor(y[1][:].rearrange("p (h e) -> p h e", h=H),
                                      ring(f"ot_{g}")[:, 0:D].rearrange("p (h e) -> p h e", h=H),
                                      inv_sum[1][:].unsqueeze(2).to_broadcast([P, H, HD]), ALU.mult
                                      ).then_inc(y1_att_done, 1)

            def values_out(layer, q, g):
                if q.valid():
                    dve.wait_ge(v_done[layer], q.count(1, g, 1))
                    dve.wait_ge(pv_done[layer], q.plus(-2).count(C, g, C))
                    dve.tensor_tensor(v[layer][q.parity][:, g, :], ring(f"v{layer}_{g}")[:, 0:D], bv_row[layer][:],
                                      ALU.add).then_inc(v_out[layer], 1)

            def inverse_sums0(q, g):
                if q.valid():
                    dve.wait_ge(exp_done[0], q.count(H, g, H))
                    dve.reciprocal(inv_raw0[:], row_sum[0][:]).then_inc(inv0_steps, 1)
                    dve.wait_ge(absmax_done, q.count(1, g, 1))
                    dve.wait_ge(probn_done, q.count(C, g, 0))
                    dve.wait_ge(inv0_steps, q.count(2, g, 1))
                    dve.scalar_tensor_tensor(out=inv_sum[0][:], in0=abs_max0[:], scalar=0.0, in1=inv_raw0[:],
                                             op0=ALU.is_gt, op1=ALU.mult).then_inc(inv0_steps, 1)

            def norm_input1(q, g):
                if q.valid():
                    dve.wait_ge(y1_done, q.count(1, g, 1))
                    norm_stats_of(1, q, g)

            def norm_apply1(q, g):
                if q.valid():
                    dve.wait_ge(rstd_steps[1], q.count(2, g, 2))
                    dve.wait_ge(stored[g], q.count(8, 0, 0))
                    dve.tensor_scalar(x2[g][:], y[1][:], mean_var[1][:, 0:1], rstd[1][:],
                                      ALU.subtract, ALU.mult).then_inc(x2_done, 1)

            def body(r, off):
                n = Pair(r, off)
                nxt, prev, prev2 = n.plus(1), n.plus(-1), n.plus(-2)
                for s in range(2):
                    late, lg = (n.plus(-3), 1) if s == 0 else (prev2, 0)
                    wo, wg = (prev, 1) if s == 0 else (n, 0)
                    norm_input0(wo, wg)
                    norm_apply0(wo, wg)
                    negate(0, n, s, (0, 1))
                    probT_out(1, late, lg)
                    negate(0, n, s, (2, 3))
                    if s == 0:
                        low_xT(nxt, 0)
                        low_xT(nxt, 1)
                        low_x1T(prev, 0)
                        low_x1T(prev, 1)
                    inverse_sums1(late, lg)
                    out1T_out(late, lg)
                    abs_max(n, s)
                    attention_out1(late, lg)
                    values_out(0, nxt, s)
                    inverse_sums0(n, s)
                    negate(1, prev2, s, (0, 1))
                    probT_out(0, n, s)
                    negate(1, prev2, s, (2, 3))
                    norm_input1(late, lg)
                    low_o0T(n, s)
                    norm_apply1(late, lg)
                    values_out(1, prev, s)

            iterations(dve, body)

        @block.gpsimd
        def _(pool):
            pool.memset(neg_half[:], -0.5).then_inc(const_done, 1)
            pool.memset(ident[:], 0.0).then_inc(ident_done, 1)
            pool.wait_ge(ident_done, 1)
            pool.affine_select(out=ident[:], in_=ident[:], compare_op=ALU.not_equal, fill=1.0, base=0,
                               pattern=[[-1, P]], channel_multiplier=1).then_inc(ident_done, 1)
            pool.wait_ge(small_loaded, 16 * 6)
            pool.tensor_scalar(bq1s[:], bqk1[:, 0, :], SCALE1, None, ALU.mult).then_inc(const_done, 1)
            pool.wait_ge(const_done, 1)

            def inverse_std(layer, q, g):
                if q.valid():
                    pool.wait_ge(norm_stats[layer], q.count(2, g, 2))
                    pool.wait_ge((x1_done, x2_done)[layer], q.count(1, g, 0))
                    pool.wait_ge(rstd_steps[layer], q.count(2, g, 0))
                    pool.sem_inc(pool_passed, 1)
                    pool.tensor_scalar(var_eps[layer][:], mean_var[layer][:, 1:2], EPS, None, ALU.add
                                       ).then_inc(rstd_steps[layer], 1)
                    pool.wait_ge(rstd_steps[layer], q.count(2, g, 1))
                    pool.tensor_tensor(rstd[layer][:], var_eps[layer][:], neg_half[:], ALU.pow
                                       ).then_inc(rstd_steps[layer], 1)

            def residual0(q):
                if q.valid():
                    b = q.parity
                    pool.wait_ge(x_loaded[b], q.loads())
                    pool.wait_ge(y0_done, q.plus(-2).count(1, 1, 1))
                    for g in range(2):
                        pool.tensor_tensor(x_bo[b][:, g, :], x_in[b][:, g, :], bo_row[:], ALU.add
                                           ).then_inc(x_bo_done, 1)

            def make_bias0(q):
                if q.valid():
                    b = q.parity
                    pool.wait_ge(adj0_loaded[b], q.loads())
                    pool.wait_ge(neg_done[0], q.plus(-2).count(H, 1, H))
                    for g in range(2):
                        pool.tensor_tensor(bias[0][b][:, g, :], adj0[b][:, g, :], adj0[b][:, g, :], ALU.add
                                           ).then_inc(bias0_done, 1)

            def make_bias1(q):
                if q.valid():
                    b = q.parity
                    pool.wait_ge(adj1_loaded[b], q.loads())
                    pool.wait_ge(neg_done[1], q.plus(-2).count(H, 1, H))
                    pool.wait_ge(bias1_steps, q.count(5, 0, 0))
                    pool.sem_inc(pool_passed, 1)
                    for g in range(2):
                        pool.tensor_scalar(mask1[:, g, :], adj1[b][:, g, :], 0.0, None, ALU.is_gt).then_inc(bias1_steps, 1)
                    for g in range(2):
                        pool.tensor_scalar(linear1[:, g, :], adj1[b][:, g, :], beta_col[:], None, ALU.mult).then_inc(bias1_steps, 1)
                    pool.wait_ge(bias1_steps, q.count(5, 0, 4))
                    for g in range(2):
                        pool.tensor_tensor(linear1[:, g, :], linear1[:, g, :], mask1[:, g, :], ALU.mult).then_inc(bias1_steps, 1)
                    pool.wait_ge(bias1_steps, q.count(5, 0, 6))
                    pool.sem_inc(pool_passed, 1)
                    for g in range(2):
                        pool.tensor_scalar(mask1[:, g, :], mask1[:, g, :], 1.0, MASKED, ALU.subtract, ALU.mult).then_inc(bias1_steps, 1)
                    pool.wait_ge(bias1_steps, q.count(5, 0, 8))
                    for g in range(2):
                        pool.tensor_tensor(bias[1][b][:, g, :], linear1[:, g, :], mask1[:, g, :], ALU.add).then_inc(bias1_steps, 1)

            def keep_x1(q):
                if q.valid():
                    b = q.parity
                    pool.wait_ge(x1_done, q.count(1, 1, 1))
                    pool.wait_ge(y1_done, q.plus(-2).count(1, 1, 1))
                    pool.sem_inc(pool_passed, 1)
                    for g in range(2):
                        pool.tensor_copy(x1_late[b][:, g, :], x1[b][:, g, :]).then_inc(x1_late_done, 1)

            def residual1(q, g):
                if q.valid():
                    pool.wait_ge(y1_att_done, q.count(1, g, 1))
                    pool.wait_ge(x1_late_done, q.count(1, 1, 1))
                    pool.tensor_tensor(y[1][:], y[1][:], x1_late[q.parity][:, g, :], ALU.add
                                       ).then_inc(y1_done, 1)

            def normalise0(q, g):
                if q.valid():
                    pool.wait_ge(inv0_steps, q.count(2, g, 2))
                    for c in range(C):
                        hs = slice(HC * c, HC * (c + 1))
                        pool.tensor_tensor(prob[0][:, hs, :], prob[0][:, hs, :],
                                           inv_sum[0][:, hs].unsqueeze(2).to_broadcast([P, HC, N]), ALU.mult
                                           ).then_inc(probn_done, 1)

            def body(r, off):
                n = Pair(r, off)
                nxt, prev, prev2 = n.plus(1), n.plus(-1), n.plus(-2)
                for s in range(2):
                    late, lg = (n.plus(-3), 1) if s == 0 else (prev2, 0)
                    wo, wg = (prev, 1) if s == 0 else (n, 0)
                    inverse_std(0, wo, wg)
                    if s == 0:
                        residual0(nxt)
                        make_bias0(nxt)
                    else:
                        make_bias1(prev)
                        keep_x1(prev)
                    residual1(late, lg)
                    normalise0(n, s)
                    inverse_std(1, late, lg)

            iterations(pool, body)


_WEIGHTS = ["L0_gnn_Wq", "L0_gnn_Wk", "L0_gnn_Wv", "L0_gnn_Wo", "L1_gnn_Wq", "L1_gnn_Wk", "L1_gnn_Wv"]
_VECTORS = ["L0_gnn_bv", "L0_gnn_bo", "L1_gnn_bq", "L1_gnn_bk", "L1_gnn_bv", "L1_gnn_beta"]


def kernel(**inputs):
    import numpy as _np
    import concourse.bacc as _bacc
    from concourse import mybir as _mybir
    from concourse.bass_utils import run_bass_kernel_spmd as _run

    nc = _bacc.Bacc("TRN2", target_bir_lowering=False, num_devices=1)
    arrays = {}

    def dram(name, a):
        a = _np.ascontiguousarray(a)
        arrays[f"in_{name}_dram"] = a
        return nc.dram_tensor(f"in_{name}_dram", a.shape, _mybir.dt.from_np(a.dtype), kind="ExternalInput").ap()

    x, adj = dram("x", inputs["x"]), dram("adj", inputs["adj"])
    wts = [dram(w, inputs[w].T if w.startswith("L0") else inputs[w]) for w in _WEIGHTS]
    bv0, bo0, bq1, bk1, bv1, beta = (dram(b, _np.reshape(inputs[b], (-1,))) for b in _VECTORS)
    out = nc.dram_tensor("out_0_dram", (128, 128, 384), _mybir.dt.float32, kind="ExternalOutput").ap()
    build(nc, x, adj, wts, bv0, bo0, bq1, bk1, bv1, beta, out)
    r = _run(nc, [arrays], core_ids=[0])
    return r.results[0]["out_0_dram"]
```

```python
from contextlib import ExitStack

import concourse.bass as bass
from concourse import mybir

F32 = mybir.dt.float32
F32R = mybir.dt.float32r
ALU = mybir.AluOpType
ACT = mybir.ActivationFunctionType
AX_X = mybir.AxisListType.X

NG, N, D = 128, 128, 384
H, HD = 12, 32
P = 128
C = D // P
HC = H // C
PAIRS = NG // 2
G2 = 2 * N
EPS = 1e-5
MASKED = 9000000000000000.0
SCALE0 = float(D) ** -0.5
SCALE1 = float(HD) ** -0.5
BIG = 3.0e38

FIRST, LAST = -1, PAIRS + 2
LOOP_FROM = 3
LOOP_N = PAIRS - 3 - LOOP_FROM
assert LOOP_N % 2 == 0

BANK_HEADS = [[b, b + HC, b + 2 * HC] for b in range(HC)]

RING = (["xt0", "wo_1", "xt1", "v0_0", "pv1_1", "g0_0", "g0_1", "ot_1", "g0_2", "x1t0", "x1t1",
         "g1_0", "g1_1", "g1_2", "pv0_0", "v1_0"]
        + ["wo_0", "g0_3", "g0_4", "pv1_0", "v0_1", "g0_5", "ot_0", "g1_3", "g1_4", "g1_5",
           "pv0_1", "v1_1"])
assert len(RING) % 2 == 0
RING_BANK = {name: i % 2 for i, name in enumerate(RING)}


class Pair:

    def __init__(self, r, off):
        self.r, self.off = r, off
        self.parity = off % 2

    def plus(self, d):
        return Pair(self.r, self.off + d)

    def index(self):
        return self.r + self.off

    def count(self, per_graph, g, plus):
        value = 2 * per_graph * self.r + (per_graph * (2 * self.off + g) + plus)
        return max(value, 0) if isinstance(value, int) else value

    def loads(self):
        value = 8 * self.r + 16 * (self.off // 2 + 1)
        return max(value, 0) if isinstance(value, int) else value

    def valid(self):
        return not isinstance(self.r, int) or 0 <= self.r + self.off < PAIRS


def iterations(eng, body, after_loop=None):
    for n in range(FIRST, LOOP_FROM):
        body(0, n)
    with eng.Fori(0, LOOP_N // 2) as turn:
        for u in range(2):
            body(2 * turn, LOOP_FROM + u)
    if after_loop:
        after_loop()
    for n in range(LOOP_FROM + LOOP_N, LAST + 1):
        body(LOOP_N, n - LOOP_N)


def build(nc, x, adj, wts, bv0, bo0, bq1, bk1, bv1, beta, out):
    with ExitStack() as ctx:
        def sb(name, shape, dt=F32):
            return ctx.enter_context(nc.sbuf_tensor(name, shape, dt))

        def bank(name):
            return ctx.enter_context(nc.psum_tensor(name, [P, 512], F32))

        def sem(name):
            return ctx.enter_context(nc.semaphore(name))

        def sems(name, n=2):
            return [sem(f"{name}_{i}") for i in range(n)]

        NW = 7
        WQ0, WK0, WV0, WO0, WQ1, WK1, WV1 = range(NW)
        w_stage = [sb(f"w_stage{i}", [P, C, D]) for i in range(2)]
        w_hi = [sb(f"w_hi{i}", [P, C, D], F32R) for i in range(NW)]
        w_lo = [sb(f"w_lo{i}", [P, C, D], F32R) for i in range(NW)]
        ident = sb("ident", [P, P])
        bv_row = [sb("bv0_row", [P, D]), sb("bv1_row", [P, D])]
        bo_row = sb("bo_row", [P, D])
        bqk1 = sb("bqk1", [P, 2, C])
        bq1s = sb("bq1s", [P, C])
        beta_col = sb("beta_col", [P, 1])
        neg_half = sb("neg_half", [P, 1])
        x_in = [sb(f"x_in{b}", [P, 2, D]) for b in range(2)]
        x_bo = [sb(f"x_bo{b}", [P, 2, D]) for b in range(2)]
        adj0 = [sb(f"adj0_{b}", [P, 2, N]) for b in range(2)]
        adj1 = [sb(f"adj1_{b}", [P, 2, N]) for b in range(2)]
        bias = [[sb(f"bias{l}_{b}", [P, 2, N]) for b in range(2)] for l in range(2)]
        qT = [[sb(f"q{l}T_{b}", [P, C, G2]) for b in range(2)] for l in range(2)]
        kT = [[sb(f"k{l}T_{b}", [P, C, G2]) for b in range(2)] for l in range(2)]
        v = [[sb(f"v{l}_{b}", [P, 2, D]) for b in range(2)] for l in range(2)]
        x1 = [sb(f"x1_{b}", [P, 2, D]) for b in range(2)]
        x1_late = [sb(f"x1_late{b}", [P, 2, D]) for b in range(2)]
        xT_hi, xT_lo = sb("xT_hi", [P, C, G2], F32R), sb("xT_lo", [P, C, G2], F32R)
        x1T_hi, x1T_lo = sb("x1T_hi", [P, C, G2], F32R), sb("x1T_lo", [P, C, G2], F32R)
        neg_s = [sb(f"neg_s{l}", [P, H, N]) for l in range(2)]
        neg_max = [sb(f"neg_max{l}", [P, H]) for l in range(2)]
        prob = [sb(f"prob{l}", [P, H, N]) for l in range(2)]
        row_sum = [sb(f"row_sum{l}", [P, H]) for l in range(2)]
        inv_sum = [sb(f"inv_sum{l}", [P, H]) for l in range(2)]
        inv_raw0 = sb("inv_raw0", [P, H])
        abs_max0 = sb("abs_max0", [P, H])
        probT = [[sb(f"prob{l}T_{c}", [P, HC, N]) for c in range(C)] for l in range(2)]
        o0T_hi, o0T_lo = sb("o0T_hi", [P, C, N], F32R), sb("o0T_lo", [P, C, N], F32R)
        o1T = sb("o1T", [P, C, N])
        y = [sb(f"y{l}", [P, D]) for l in range(2)]
        stats = [sb(f"stats{l}", [P, 6]) for l in range(2)]
        mean_var = [sb(f"mean_var{l}", [P, 2]) for l in range(2)]
        var_eps = [sb(f"var_eps{l}", [P, 1]) for l in range(2)]
        rstd = [sb(f"rstd{l}", [P, 1]) for l in range(2)]
        mask1, linear1 = sb("mask1", [P, 2, N]), sb("linear1", [P, 2, N])
        x2 = [sb(f"x2_{g}", [P, D]) for g in range(2)]

        s_bank = [bank(f"s_bank{i}") for i in range(HC)]
        a_bank = [bank(f"a_bank{i}") for i in range(2)]
        t_bank = [bank(f"t_bank{i}") for i in range(2)]

        def ring(name):
            return a_bank[RING_BANK[name]]

        def t_index(layer, g, c):
            return (2 * C * (1 - g) + c if layer else 2 * C * g + C + c) % 2

        w_loaded = sems("w_loaded")
        small_loaded = sem("small_loaded")
        x_loaded, adj0_loaded, adj1_loaded = sems("x_loaded"), sems("adj0_loaded"), sems("adj1_loaded")
        x1_kept = sems("x1_kept")
        stored = sems("stored")
        w_hi_done, w_lo_done = sem("w_hi_done"), sem("w_lo_done")
        const_done = sem("const_done")
        ident_done = sem("ident_done")
        dve_passed, pool_passed = sem("dve_passed"), sem("pool_passed")
        xt_done, x1t_done = sem("xt_done"), sem("x1t_done")
        g_done = sems("g_done")
        v_done = sems("v_done")
        s_done = sems("s_done")
        pt_done = sems("pt_done")
        pv_done = sems("pv_done")
        wo_done, ot_done = sem("wo_done"), sem("ot_done")
        xt_hi_done, x1t_hi_done, o0t_hi_done = sem("xt_hi_done"), sem("x1t_hi_done"), sem("o0t_hi_done")
        g_out = sems("g_out")
        exp_done = sems("exp_done")
        xt_lo_done, x1t_lo_done, o0t_lo_done = sem("xt_lo_done"), sem("x1t_lo_done"), sem("o0t_lo_done")
        v_out = sems("v_out")
        o1t_out = sem("o1t_out")
        neg_done = sems("neg_done")
        absmax_done = sem("absmax_done")
        inv0_steps = sem("inv0_steps")
        inv1_done = sem("inv1_done")
        y0_done, y1_att_done = sem("y0_done"), sem("y1_att_done")
        norm_stats = sems("norm_stats")
        x1_done, x2_done = sem("x1_done"), sem("x2_done")
        x_bo_done, bias0_done, bias1_steps = sem("x_bo_done"), sem("bias0_done"), sem("bias1_steps")
        rstd_steps = sems("rstd_steps")
        probn_done = sem("probn_done")
        y1_done = sem("y1_done")
        pt_out = [sems(f"pt{l}_out", C) for l in range(2)]

        block = ctx.enter_context(nc.Block())

        @block.sync
        def _(sp):
            def load_x(q):
                if q.valid():
                    b = q.parity
                    sp.wait_ge(xt_done, q.plus(-2).count(1, 1, 1))
                    sp.wait_ge(x_bo_done, q.plus(-2).count(1, 1, 1))
                    sp.dma_start(x_in[b][:], x[bass.ds(2 * q.index(), 2)].rearrange("g n d -> n g d")
                                 ).then_inc(x_loaded[b], 16)
                    sp.wait_ge(bias0_done, q.plus(-2).count(1, 1, 1))
                    sp.dma_start(adj0[b][:], adj[bass.ds(2 * q.index(), 2)].rearrange("g n k -> n g k")
                                 ).then_inc(adj0_loaded[b], 16)

            def load_adj1(q):
                if q.valid():
                    b = q.parity
                    sp.wait_ge(bias1_steps, q.plus(-2).count(5, 1, 5))
                    sp.dma_start(adj1[b][:], adj[bass.ds(2 * q.index(), 2)].rearrange("g n k -> n g k")
                                 ).then_inc(adj1_loaded[b], 16)

            def store(q, g):
                if q.valid():
                    sp.wait_ge(x2_done, q.count(1, g, 1))
                    sp.dma_start(out[bass.ds(2 * q.index() + g, 1)].rearrange("g n d -> n (g d)"), x2[g][:]
                                 ).then_inc(stored[g], 16)

            def keep_x1(q):
                if q.valid():
                    b = q.parity
                    sp.wait_ge(x1_done, q.count(1, 1, 1))
                    sp.wait_ge(y1_done, q.plus(-2).count(1, 1, 1))
                    sp.dma_start(x1_late[b][:], x1[b][:]).then_inc(x1_kept[b], 16)

            load_x(Pair(0, 0))
            for i in range(NW):
                sp.wait_ge(w_lo_done, max(i - 1, 0))
                sp.dma_start(w_stage[i % 2][:], wts[i].rearrange("(c p) o -> p c o", p=P)
                             ).then_inc(w_loaded[i % 2], 16)
                if i == 1:
                    sp.dma_start(bv_row[0][:], bv0.partition_broadcast(P)).then_inc(small_loaded, 16)
                    sp.dma_start(bv_row[1][:], bv1.partition_broadcast(P)).then_inc(small_loaded, 16)
                    sp.dma_start(bo_row[:], bo0.partition_broadcast(P)).then_inc(small_loaded, 16)
                    sp.dma_start(beta_col[:], beta.partition_broadcast(P)).then_inc(small_loaded, 16)
                    for j, b_ in enumerate((bq1, bk1)):
                        sp.dma_start(bqk1[:, j, :], b_.rearrange("(c p) -> p c", p=P),
                                     allow_slow_non_contiguous=True).then_inc(small_loaded, 16)
            load_x(Pair(0, 1))

            def body(r, off):
                n = Pair(r, off)
                load_x(n.plus(3))
                store(n.plus(-3), 1)
                keep_x1(n.plus(-1))
                load_adj1(n.plus(1))
                store(n.plus(-2), 0)

            iterations(sp, body)
            for g in range(2):
                sp.wait_ge(stored[g], 16 * PAIRS)

        @block.tensor
        def _(pe):
            a_read = [(xt_lo_done, 0, 0, 0, 0)] * 2
            s_read = [(neg_done[0], 0, 0, 0, 0)] * HC
            t_read = [(exp_done[1], 0, 0, 0, 0)] * 2

            def last_read(table, i, r):
                sem_, off, per, g, plus = table[i]
                return sem_, Pair(r, off).count(per, g, plus)

            def after_loop():
                for table in (a_read, s_read, t_read):
                    for i, (sem_, off, per, g, plus) in enumerate(table):
                        table[i] = (sem_, off - 2, per, g, plus)

            def transpose_x(q, g, r):
                if q.valid():
                    pe.wait_ge(*last_read(a_read, RING_BANK[f"xt{g}"], r))
                    a_read[RING_BANK[f"xt{g}"]] = (xt_lo_done, q.off, 1, g, 1)
                    pe.wait_ge(x_loaded[q.parity], q.loads())
                    for c in range(C):
                        mm = pe.transpose(ring(f"xt{g}")[:, c * P:(c + 1) * P],
                                          x_in[q.parity][:, g, c * P:(c + 1) * P], ident[:])
                    mm.then_inc(xt_done, 1)

            def transpose_x1(q, g, r):
                if q.valid():
                    pe.wait_ge(*last_read(a_read, RING_BANK[f"x1t{g}"], r))
                    a_read[RING_BANK[f"x1t{g}"]] = (x1t_lo_done, q.off, 1, g, 1)
                    pe.wait_ge(x1_done, q.count(1, g, 1))
                    for c in range(C):
                        mm = pe.transpose(ring(f"x1t{g}")[:, c * P:(c + 1) * P],
                                          x1[q.parity][:, g, c * P:(c + 1) * P], ident[:])
                    mm.then_inc(x1t_done, 1)

            def split_product(dst, a_hi, a_lo, b_hi, b_lo):
                for c in range(C):
                    pe.matmul(dst, a_hi(c), b_hi(c), start=(c == 0), stop=False)
                    pe.matmul(dst, a_hi(c), b_lo(c), start=False, stop=False)
                    mm = pe.matmul(dst, a_lo(c), b_hi(c), start=False, stop=(c == C - 1))
                return mm

            t_hi, t_lo = (xT_hi, x1T_hi), (xT_lo, x1T_lo)
            lo_done = (xt_lo_done, x1t_lo_done)

            def project_qk(layer, q, j, r):
                if q.valid():
                    name = f"g{layer}_{j}"
                    pe.wait_ge(*last_read(a_read, RING_BANK[name], r))
                    a_read[RING_BANK[name]] = (g_out[layer], q.off, 3, 0, j + 1)
                    pe.wait_ge(lo_done[layer], q.count(1, 1, 1))
                    wi = ((WQ0, WK0), (WQ1, WK1))[layer][j // C]
                    if q.off == 0 and isinstance(r, int) and r == 0:
                        pe.wait_ge(w_lo_done, wi + 1)
                    f = slice((j % C) * P, (j % C + 1) * P)
                    split_product(ring(name)[:, 0:G2], lambda c: w_hi[wi][:, c, f], lambda c: w_lo[wi][:, c, f],
                                  lambda c: t_hi[layer][:, c, :], lambda c: t_lo[layer][:, c, :]
                                  ).then_inc(g_done[layer], 1)

            def project_v(layer, q, g, r):
                if q.valid():
                    name = f"v{layer}_{g}"
                    pe.wait_ge(*last_read(a_read, RING_BANK[name], r))
                    a_read[RING_BANK[name]] = (v_out[layer], q.off, 1, g, 1)
                    wi = (WV0, WV1)[layer]
                    if q.off == 0 and isinstance(r, int) and r == 0:
                        pe.wait_ge(w_lo_done, wi + 1)
                    m = slice(g * N, (g + 1) * N)
                    split_product(ring(name)[:, 0:D], lambda c: t_hi[layer][:, c, m], lambda c: t_lo[layer][:, c, m],
                                  lambda c: w_hi[wi][:, c, :], lambda c: w_lo[wi][:, c, :]
                                  ).then_inc(v_done[layer], 1)

            def scores(layer, q, g, r):
                if q.valid():
                    pe.wait_ge(g_out[layer], q.count(3, 1, 3))
                    m = slice(g * N, (g + 1) * N)
                    for h in range(H):
                        c, j = divmod(h, HC)
                        if c == 0:
                            pe.wait_ge(*last_read(s_read, j, r))
                            s_read[j] = (neg_done[layer], q.off, H, g, C * (j + 1))
                        rows = slice(HD * j, HD * (j + 1))
                        mm = pe.matmul(s_bank[j][:, c * N:(c + 1) * N], qT[layer][q.parity][rows, c, m],
                                       kT[layer][q.parity][rows, c, m], start=True, stop=True)
                        if c == C - 1:
                            mm.then_inc(s_done[layer], 1)

            def transpose_probs(layer, q, g, c, r):
                if q.valid():
                    i = t_index(layer, g, c)
                    pe.wait_ge(*last_read(t_read, i, r))
                    t_read[i] = (pt_out[layer][c], q.off, 1, g, 1)
                    if layer == 0:
                        pe.wait_ge(probn_done, q.count(C, g, c + 1))
                    else:
                        pe.wait_ge(exp_done[1], q.count(H, g, H))
                    for j in range(HC):
                        mm = pe.transpose(t_bank[i][:, j * N:(j + 1) * N], prob[layer][:, HC * c + j, :], ident[:])
                    mm.then_inc(pt_done[layer], 1)

            def attend(layer, q, g, r):
                if q.valid():
                    name = f"pv{layer}_{g}"
                    pe.wait_ge(*last_read(a_read, RING_BANK[name], r))
                    a_read[RING_BANK[name]] = ((o0t_lo_done, o1t_out)[layer], q.off, 1, g, 1)
                    pe.wait_ge(v_out[layer], q.count(1, g, 1))
                    for c in range(C):
                        pe.wait_ge(pt_out[layer][c], q.count(1, g, 1))
                        for j in range(HC):
                            f = slice(HD * (HC * c + j), HD * (HC * c + j + 1))
                            mm = pe.matmul(ring(name)[HD * j:HD * (j + 1), c * N:(c + 1) * N],
                                           v[layer][q.parity][:, g, f], probT[layer][c][:, j, :],
                                           start=True, stop=True)
                        mm.then_inc(pv_done[layer], 1)

            def transpose_out1(q, g, r):
                if q.valid():
                    name = f"ot_{g}"
                    pe.wait_ge(*last_read(a_read, RING_BANK[name], r))
                    a_read[RING_BANK[name]] = (y1_att_done, q.off, 1, g, 1)
                    pe.wait_ge(o1t_out, q.count(1, g, 1))
                    for c in range(C):
                        mm = pe.transpose(ring(name)[:, c * P:(c + 1) * P], o1T[:, c, :], ident[:])
                    mm.then_inc(ot_done, 1)

            def project_out0(q, g, r):
                if q.valid():
                    name = f"wo_{g}"
                    pe.wait_ge(*last_read(a_read, RING_BANK[name], r))
                    a_read[RING_BANK[name]] = (y0_done, q.off, 1, g, 1)
                    pe.wait_ge(o0t_lo_done, q.count(1, g, 1))
                    if q.off == 0 and isinstance(r, int) and r == 0:
                        pe.wait_ge(w_lo_done, WO0 + 1)
                    split_product(ring(name)[:, 0:D], lambda c: o0T_hi[:, c, :], lambda c: o0T_lo[:, c, :],
                                  lambda c: w_hi[WO0][:, c, :], lambda c: w_lo[WO0][:, c, :]
                                  ).then_inc(wo_done, 1)

            pe.wait_ge(ident_done, 2)

            def body(r, off):
                n = Pair(r, off)
                nxt, prev, prev2, prev3 = n.plus(1), n.plus(-1), n.plus(-2), n.plus(-3)
                scores(0, n, 0, r)
                transpose_x(nxt, 0, r)
                project_out0(prev, 1, r)
                transpose_probs(1, prev3, 1, 0, r)
                transpose_probs(1, prev3, 1, 1, r)
                transpose_x(nxt, 1, r)
                transpose_probs(1, prev3, 1, 2, r)
                project_v(0, nxt, 0, r)
                attend(1, prev3, 1, r)
                project_qk(0, nxt, 0, r)
                project_qk(0, nxt, 1, r)
                transpose_out1(prev3, 1, r)
                project_qk(0, nxt, 2, r)
                transpose_x1(prev, 0, r)
                transpose_x1(prev, 1, r)
                scores_and_layer1_part(n, prev, prev2, 0, r)
                scores(0, n, 1, r)
                project_out0(n, 0, r)
                transpose_probs(1, prev2, 0, 0, r)
                transpose_probs(1, prev2, 0, 1, r)
                project_qk(0, nxt, 3, r)
                transpose_probs(1, prev2, 0, 2, r)
                project_qk(0, nxt, 4, r)
                attend(1, prev2, 0, r)
                project_v(0, nxt, 1, r)
                project_qk(0, nxt, 5, r)
                transpose_out1(prev2, 0, r)
                scores_and_layer1_part(n, prev, prev2, 1, r)

            def scores_and_layer1_part(n, prev, prev2, g, r):
                scores(1, prev2, g, r)
                project_qk(1, prev, 3 * g, r)
                transpose_probs(0, n, g, 0, r)
                transpose_probs(0, n, g, 1, r)
                project_qk(1, prev, 3 * g + 1, r)
                transpose_probs(0, n, g, 2, r)
                project_qk(1, prev, 3 * g + 2, r)
                attend(0, n, g, r)
                project_v(1, prev, g, r)

            iterations(pe, body, after_loop)

        @block.scalar
        def _(act):
            for i in range(NW):
                act.wait_ge(w_loaded[i % 2], 16 * (i // 2 + 1))
                act.activation(w_hi[i][:], w_stage[i % 2][:], ACT.Copy).then_inc(w_hi_done, 1)

            def high_xT(q, g):
                if q.valid():
                    act.wait_ge(xt_done, q.count(1, g, 1))
                    if g == 0:
                        act.wait_ge(v_done[0], q.count(1, 0, 0))
                    act.activation(xT_hi[:, :, g * N:(g + 1) * N],
                                   ring(f"xt{g}")[:, 0:D].rearrange("p (c n) -> p c n", c=C), ACT.Copy
                                   ).then_inc(xt_hi_done, 1)

            def high_x1T(q, g):
                if q.valid():
                    act.wait_ge(x1t_done, q.count(1, g, 1))
                    if g == 0:
                        act.wait_ge(v_done[1], q.count(1, 0, 0))
                    act.activation(x1T_hi[:, :, g * N:(g + 1) * N],
                                   ring(f"x1t{g}")[:, 0:D].rearrange("p (c n) -> p c n", c=C), ACT.Copy
                                   ).then_inc(x1t_hi_done, 1)

            def high_o0T(q, g):
                if q.valid():
                    act.wait_ge(pv_done[0], q.count(C, g, C))
                    act.wait_ge(wo_done, q.count(1, g, 0))
                    act.activation(o0T_hi[:], ring(f"pv0_{g}")[:, 0:D].rearrange("p (c n) -> p c n", c=C),
                                   ACT.Copy).then_inc(o0t_hi_done, 1)

            def qk_out(layer, q, j):
                if q.valid():
                    b, c = q.parity, j % C
                    act.wait_ge(g_done[layer], q.count(3, 0, j + 1))
                    act.wait_ge(s_done[layer], q.plus(-2).count(HC, 1, HC))
                    src = ring(f"g{layer}_{j}")[:, 0:G2]
                    if layer == 0:
                        dst = (qT if j < C else kT)[0][b][:, c, :]
                        ins = act.activation(dst, src, ACT.Copy, scale=SCALE0 if j < C else 1.0)
                    elif j < C:
                        ins = act.activation(qT[1][b][:, c, :], src, ACT.Identity, bias=bq1s[:, c:c + 1], scale=SCALE1)
                    else:
                        ins = act.activation(kT[1][b][:, c, :], src, ACT.Identity, bias=bqk1[:, 1, c:c + 1])
                    ins.then_inc(g_out[layer], 1)

            def probT_out(layer, q, g, c):
                if q.valid():
                    act.wait_ge(pt_done[layer], q.count(C, g, c + 1))
                    act.wait_ge(pv_done[layer], q.count(C, g, c + 1 - C))
                    act.activation(probT[layer][c][:],
                                   t_bank[t_index(layer, g, c)][:].rearrange("p (j n) -> p j n", j=HC), ACT.Copy
                                   ).then_inc(pt_out[layer][c], 1)

            def exps(layer, q, g, b):
                if q.valid():
                    if b == 0:
                        act.wait_ge(pt_done[layer], q.count(C, g, 0))
                        if layer == 1:
                            act.wait_ge(inv1_done, q.count(1, g, 0))
                    for i, h in enumerate(BANK_HEADS[b]):
                        act.wait_ge(neg_done[layer], q.count(H, g, C * b + i + 1))
                        act.activation(prob[layer][:, h, :], neg_s[layer][:, h, :], ACT.Exp,
                                       bias=neg_max[layer][:, h:h + 1], scale=-1.0,
                                       accum_out=row_sum[layer][:, h:h + 1]).then_inc(exp_done[layer], 1)

            act.wait_ge(const_done, 2)
            act.wait_ge(small_loaded, 16 * 6)

            def body(r, off):
                n = Pair(r, off)
                nxt, prev, prev2, prev3 = n.plus(1), n.plus(-1), n.plus(-2), n.plus(-3)
                exps(0, n, 0, 0)
                high_xT(nxt, 0)
                exps(0, n, 0, 1)
                probT_out(1, prev3, 1, 0)
                high_xT(nxt, 1)
                probT_out(1, prev3, 1, 2)
                exps(0, n, 0, 2)
                exps(0, n, 0, 3)
                qk_out(0, nxt, 0)
                qk_out(0, nxt, 1)
                qk_out(0, nxt, 2)
                high_x1T(prev, 0)
                high_x1T(prev, 1)
                layer1_part(n, prev, prev2, 0)
                exps(0, n, 1, 0)
                exps(0, n, 1, 1)
                probT_out(1, prev2, 0, 0)
                qk_out(0, nxt, 3)
                probT_out(1, prev2, 0, 2)
                exps(0, n, 1, 2)
                qk_out(0, nxt, 4)
                exps(0, n, 1, 3)
                qk_out(0, nxt, 5)
                layer1_part(n, prev, prev2, 1)

            def layer1_part(n, prev, prev2, g):
                exps(1, prev2, g, 0)
                qk_out(1, prev, 3 * g)
                probT_out(0, n, g, 0)
                exps(1, prev2, g, 1)
                qk_out(1, prev, 3 * g + 1)
                probT_out(0, n, g, 2)
                exps(1, prev2, g, 2)
                qk_out(1, prev, 3 * g + 2)
                high_o0T(n, g)
                exps(1, prev2, g, 3)

            iterations(act, body)

        @block.vector
        def _(dve):
            for i in range(NW):
                dve.wait_ge(w_hi_done, i + 1)
                dve.tensor_tensor(w_lo[i][:], w_stage[i % 2][:], w_hi[i][:].bitcast(F32), ALU.subtract
                                  ).then_inc(w_lo_done, 1)
            dve.wait_ge(small_loaded, 16 * 6)

            def add_residual0(q, g):
                if q.valid():
                    dve.wait_ge(wo_done, q.count(1, g, 1))
                    dve.wait_ge(x_bo_done, q.count(1, 1, 1))
                    dve.wait_ge(x1_done, q.count(1, g, 0))
                    dve.tensor_tensor(y[0][:], ring(f"wo_{g}")[:, 0:D], x_bo[q.parity][:, g, :], ALU.add
                                      ).then_inc(y0_done, 1)

            def norm_input0(q, g):
                if q.valid():
                    dve.wait_ge(y0_done, q.count(1, g, 1))
                    norm_stats_of(0, q, g)

            def norm_stats_of(layer, q, g):
                dve.bn_stats(stats[layer][:], y[layer][:]).then_inc(norm_stats[layer], 1)
                dve.wait_ge(norm_stats[layer], q.count(2, g, 1))
                dve.sem_inc(dve_passed, 1)
                dve.bn_aggr(mean_var[layer][:], stats[layer][:]).then_inc(norm_stats[layer], 1)

            def norm_apply0(q, g):
                if q.valid():
                    dve.wait_ge(rstd_steps[0], q.count(2, g, 2))
                    dve.wait_ge(x1t_done, q.plus(-2).count(1, g, 1))
                    dve.wait_ge(x1_kept[q.parity], q.plus(-2).loads())
                    dve.tensor_scalar(x1[q.parity][:, g, :], y[0][:], mean_var[0][:, 0:1], rstd[0][:],
                                      ALU.subtract, ALU.mult).then_inc(x1_done, 1)

            def negate(layer, q, g, banks):
                if q.valid():
                    for b in banks:
                        if b == 0:
                            if layer == 0:
                                dve.wait_ge(bias0_done, q.count(1, 1, 1))
                                dve.wait_ge(absmax_done, q.count(1, g, 0))
                            else:
                                dve.wait_ge(bias1_steps, q.count(5, 1, 5))
                            dve.wait_ge(exp_done[layer], q.count(H, g, 0))
                        dve.wait_ge(s_done[layer], q.count(HC, g, b + 1))
                        dve.sem_inc(dve_passed, 1)
                        for h in BANK_HEADS[b]:
                            dve.tensor_tensor_reduce(neg_s[layer][:, h, :],
                                                     s_bank[b][:, (h // HC) * N:(h // HC + 1) * N],
                                                     bias[layer][q.parity][:, g, :], -1.0, BIG, ALU.add, ALU.min,
                                                     neg_max[layer][:, h:h + 1]).then_inc(neg_done[layer], 1)

            def probT_out(layer, q, g):
                if q.valid():
                    dve.wait_ge(pt_done[layer], q.count(C, g, 2))
                    dve.wait_ge(pv_done[layer], q.count(C, g, 2 - C))
                    dve.tensor_copy(probT[layer][1][:],
                                    t_bank[t_index(layer, g, 1)][:].rearrange("p (j n) -> p j n", j=HC)
                                    ).then_inc(pt_out[layer][1], 1)

            def low_part(dst, name, hi, hi_done, done, q, g):
                dve.wait_ge(hi_done, q.count(1, g, 1))
                dve.tensor_tensor(dst, ring(name)[:, 0:D].rearrange("p (c n) -> p c n", c=C), hi.bitcast(F32),
                                  ALU.subtract).then_inc(done, 1)

            def low_xT(q, g):
                if q.valid():
                    if g == 0:
                        dve.wait_ge(v_done[0], q.count(1, 0, 0))
                    m = slice(g * N, (g + 1) * N)
                    low_part(xT_lo[:, :, m], f"xt{g}", xT_hi[:, :, m], xt_hi_done, xt_lo_done, q, g)

            def low_x1T(q, g):
                if q.valid():
                    if g == 0:
                        dve.wait_ge(v_done[1], q.count(1, 0, 0))
                    m = slice(g * N, (g + 1) * N)
                    low_part(x1T_lo[:, :, m], f"x1t{g}", x1T_hi[:, :, m], x1t_hi_done, x1t_lo_done, q, g)

            def low_o0T(q, g):
                if q.valid():
                    dve.wait_ge(wo_done, q.count(1, g, 0))
                    low_part(o0T_lo[:], f"pv0_{g}", o0T_hi[:], o0t_hi_done, o0t_lo_done, q, g)

            def out1T_out(q, g):
                if q.valid():
                    dve.wait_ge(pv_done[1], q.count(C, g, C))
                    dve.wait_ge(ot_done, q.count(1, g, 0))
                    dve.tensor_copy(o1T[:], ring(f"pv1_{g}")[:, 0:D].rearrange("p (c n) -> p c n", c=C)
                                    ).then_inc(o1t_out, 1)

            def abs_max(q, g):
                if q.valid():
                    dve.wait_ge(neg_done[0], q.count(H, g, H))
                    dve.wait_ge(inv0_steps, q.count(2, g, 0))
                    dve.tensor_reduce(abs_max0[:], neg_s[0][:], AX_X, ALU.max, apply_absolute_value=True
                                      ).then_inc(absmax_done, 1)

            def inverse_sums1(q, g):
                if q.valid():
                    dve.wait_ge(exp_done[1], q.count(H, g, H))
                    dve.wait_ge(y1_att_done, q.count(1, g, 0))
                    dve.reciprocal(inv_sum[1][:], row_sum[1][:]).then_inc(inv1_done, 1)

            def attention_out1(q, g):
                if q.valid():
                    dve.wait_ge(ot_done, q.count(1, g, 1))
                    dve.wait_ge(inv1_done, q.count(1, g, 1))
                    dve.wait_ge(x2_done, q.count(1, g, 0))
                    dve.tensor_tensor(y[1][:].rearrange("p (h e) -> p h e", h=H),
                                      ring(f"ot_{g}")[:, 0:D].rearrange("p (h e) -> p h e", h=H),
                                      inv_sum[1][:].unsqueeze(2).to_broadcast([P, H, HD]), ALU.mult
                                      ).then_inc(y1_att_done, 1)

            def values_out(layer, q, g):
                if q.valid():
                    dve.wait_ge(v_done[layer], q.count(1, g, 1))
                    dve.wait_ge(pv_done[layer], q.plus(-2).count(C, g, C))
                    dve.tensor_tensor(v[layer][q.parity][:, g, :], ring(f"v{layer}_{g}")[:, 0:D], bv_row[layer][:],
                                      ALU.add).then_inc(v_out[layer], 1)

            def inverse_sums0(q, g):
                if q.valid():
                    dve.wait_ge(exp_done[0], q.count(H, g, H))
                    dve.reciprocal(inv_raw0[:], row_sum[0][:]).then_inc(inv0_steps, 1)
                    dve.wait_ge(absmax_done, q.count(1, g, 1))
                    dve.wait_ge(probn_done, q.count(C, g, 0))
                    dve.wait_ge(inv0_steps, q.count(2, g, 1))
                    dve.scalar_tensor_tensor(out=inv_sum[0][:], in0=abs_max0[:], scalar=0.0, in1=inv_raw0[:],
                                             op0=ALU.is_gt, op1=ALU.mult).then_inc(inv0_steps, 1)

            def norm_input1(q, g):
                if q.valid():
                    dve.wait_ge(y1_done, q.count(1, g, 1))
                    norm_stats_of(1, q, g)

            def norm_apply1(q, g):
                if q.valid():
                    dve.wait_ge(rstd_steps[1], q.count(2, g, 2))
                    dve.wait_ge(stored[g], q.count(8, 0, 0))
                    dve.tensor_scalar(x2[g][:], y[1][:], mean_var[1][:, 0:1], rstd[1][:],
                                      ALU.subtract, ALU.mult).then_inc(x2_done, 1)

            def body(r, off):
                n = Pair(r, off)
                nxt, prev, prev2 = n.plus(1), n.plus(-1), n.plus(-2)
                for s in range(2):
                    late0, late1, lg = (prev, n.plus(-3), 1) if s == 0 else (n, prev2, 0)
                    negate(0, n, s, (0, 1))
                    if s == 0:
                        low_xT(nxt, 0)
                    negate(0, n, s, (2, 3))
                    add_residual0(late0, lg)
                    probT_out(1, late1, lg)
                    if s == 0:
                        low_xT(nxt, 1)
                        norm_input0(late0, lg)
                        values_out(0, nxt, s)
                        out1T_out(late1, lg)
                    else:
                        norm_input0(late0, lg)
                        out1T_out(late1, lg)
                        values_out(0, nxt, s)
                    norm_apply0(late0, lg)
                    abs_max(n, s)
                    inverse_sums1(late1, lg)
                    inverse_sums0(n, s)
                    attention_out1(late1, lg)
                    if s == 0:
                        low_x1T(prev, 0)
                        low_x1T(prev, 1)
                    negate(1, prev2, s, (0, 1, 2, 3))
                    norm_input1(late1, lg)
                    probT_out(0, n, s)
                    norm_apply1(late1, lg)
                    low_o0T(n, s)
                    values_out(1, prev, s)

            iterations(dve, body)

        @block.gpsimd
        def _(pool):
            pool.memset(neg_half[:], -0.5).then_inc(const_done, 1)
            pool.memset(ident[:], 0.0).then_inc(ident_done, 1)
            pool.wait_ge(ident_done, 1)
            pool.affine_select(out=ident[:], in_=ident[:], compare_op=ALU.not_equal, fill=1.0, base=0,
                               pattern=[[-1, P]], channel_multiplier=1).then_inc(ident_done, 1)
            pool.wait_ge(small_loaded, 16 * 6)
            pool.tensor_scalar(bq1s[:], bqk1[:, 0, :], SCALE1, None, ALU.mult).then_inc(const_done, 1)
            pool.wait_ge(const_done, 1)

            def inverse_std(layer, q, g):
                if q.valid():
                    pool.wait_ge(norm_stats[layer], q.count(2, g, 2))
                    pool.wait_ge((x1_done, x2_done)[layer], q.count(1, g, 0))
                    pool.wait_ge(rstd_steps[layer], q.count(2, g, 0))
                    pool.sem_inc(pool_passed, 1)
                    pool.tensor_scalar(var_eps[layer][:], mean_var[layer][:, 1:2], EPS, None, ALU.add
                                       ).then_inc(rstd_steps[layer], 1)
                    pool.wait_ge(rstd_steps[layer], q.count(2, g, 1))
                    pool.tensor_tensor(rstd[layer][:], var_eps[layer][:], neg_half[:], ALU.pow
                                       ).then_inc(rstd_steps[layer], 1)

            def residual0(q):
                if q.valid():
                    b = q.parity
                    pool.wait_ge(x_loaded[b], q.loads())
                    pool.wait_ge(y0_done, q.plus(-2).count(1, 1, 1))
                    for g in range(2):
                        pool.tensor_tensor(x_bo[b][:, g, :], x_in[b][:, g, :], bo_row[:], ALU.add
                                           ).then_inc(x_bo_done, 1)

            def make_bias0(q):
                if q.valid():
                    b = q.parity
                    pool.wait_ge(adj0_loaded[b], q.loads())
                    pool.wait_ge(neg_done[0], q.plus(-2).count(H, 1, H))
                    for g in range(2):
                        pool.tensor_tensor(bias[0][b][:, g, :], adj0[b][:, g, :], adj0[b][:, g, :], ALU.add
                                           ).then_inc(bias0_done, 1)

            def make_bias1(q):
                if q.valid():
                    b = q.parity
                    pool.wait_ge(adj1_loaded[b], q.loads())
                    pool.wait_ge(neg_done[1], q.plus(-2).count(H, 1, H))
                    pool.wait_ge(bias1_steps, q.count(5, 0, 0))
                    pool.sem_inc(pool_passed, 1)
                    for g in range(2):
                        pool.tensor_scalar(mask1[:, g, :], adj1[b][:, g, :], 0.0, None, ALU.is_gt).then_inc(bias1_steps, 1)
                    for g in range(2):
                        pool.tensor_scalar(linear1[:, g, :], adj1[b][:, g, :], beta_col[:], None, ALU.mult).then_inc(bias1_steps, 1)
                    pool.wait_ge(bias1_steps, q.count(5, 0, 4))
                    for g in range(2):
                        pool.tensor_tensor(linear1[:, g, :], linear1[:, g, :], mask1[:, g, :], ALU.mult).then_inc(bias1_steps, 1)
                    pool.wait_ge(bias1_steps, q.count(5, 0, 6))
                    pool.sem_inc(pool_passed, 1)
                    for g in range(2):
                        pool.tensor_scalar(mask1[:, g, :], mask1[:, g, :], 1.0, MASKED, ALU.subtract, ALU.mult).then_inc(bias1_steps, 1)
                    pool.wait_ge(bias1_steps, q.count(5, 0, 8))
                    for g in range(2):
                        pool.tensor_tensor(bias[1][b][:, g, :], linear1[:, g, :], mask1[:, g, :], ALU.add).then_inc(bias1_steps, 1)

            def residual1(q, g):
                if q.valid():
                    pool.wait_ge(y1_att_done, q.count(1, g, 1))
                    pool.wait_ge(x1_kept[q.parity], q.loads())
                    pool.tensor_tensor(y[1][:], y[1][:], x1_late[q.parity][:, g, :], ALU.add
                                       ).then_inc(y1_done, 1)

            def normalise0(q, g):
                if q.valid():
                    pool.wait_ge(inv0_steps, q.count(2, g, 2))
                    for c in range(C):
                        hs = slice(HC * c, HC * (c + 1))
                        pool.tensor_tensor(prob[0][:, hs, :], prob[0][:, hs, :],
                                           inv_sum[0][:, hs].unsqueeze(2).to_broadcast([P, HC, N]), ALU.mult
                                           ).then_inc(probn_done, 1)

            def body(r, off):
                n = Pair(r, off)
                nxt, prev, prev2 = n.plus(1), n.plus(-1), n.plus(-2)
                for s in range(2):
                    late0, late1, lg = (prev, n.plus(-3), 1) if s == 0 else (n, prev2, 0)
                    inverse_std(0, late0, lg)
                    if s == 0:
                        residual0(nxt)
                        make_bias0(nxt)
                    normalise0(n, s)
                    residual1(late1, lg)
                    inverse_std(1, late1, lg)
                    if s == 1:
                        make_bias1(prev)

            iterations(pool, body)


_WEIGHTS = ["L0_gnn_Wq", "L0_gnn_Wk", "L0_gnn_Wv", "L0_gnn_Wo", "L1_gnn_Wq", "L1_gnn_Wk", "L1_gnn_Wv"]
_VECTORS = ["L0_gnn_bv", "L0_gnn_bo", "L1_gnn_bq", "L1_gnn_bk", "L1_gnn_bv", "L1_gnn_beta"]


def kernel(**inputs):
    import numpy as _np
    import concourse.bacc as _bacc
    from concourse import mybir as _mybir
    from concourse.bass_utils import run_bass_kernel_spmd as _run

    nc = _bacc.Bacc("TRN2", target_bir_lowering=False, num_devices=1)
    arrays = {}

    def dram(name, a):
        a = _np.ascontiguousarray(a)
        arrays[f"in_{name}_dram"] = a
        return nc.dram_tensor(f"in_{name}_dram", a.shape, _mybir.dt.from_np(a.dtype), kind="ExternalInput").ap()

    x, adj = dram("x", inputs["x"]), dram("adj", inputs["adj"])
    wts = [dram(w, inputs[w].T if w.startswith("L0") else inputs[w]) for w in _WEIGHTS]
    bv0, bo0, bq1, bk1, bv1, beta = (dram(b, _np.reshape(inputs[b], (-1,))) for b in _VECTORS)
    out = nc.dram_tensor("out_0_dram", (128, 128, 384), _mybir.dt.float32, kind="ExternalOutput").ap()
    build(nc, x, adj, wts, bv0, bo0, bq1, bk1, bv1, beta, out)
    r = _run(nc, [arrays], core_ids=[0])
    return r.results[0]["out_0_dram"]
```

```python
from contextlib import ExitStack

import concourse.bass as bass
from concourse import mybir

F32 = mybir.dt.float32
F32R = mybir.dt.float32r
ALU = mybir.AluOpType
ACT = mybir.ActivationFunctionType
AX_X = mybir.AxisListType.X

NG, N, D = 128, 128, 384
H, HD = 12, 32
P = 128
C = D // P
HC = H // C
PAIRS = NG // 2
G2 = 2 * N
EPS = 1e-5
MASKED = 9000000000000000.0
SCALE0 = float(D) ** -0.5
SCALE1 = float(HD) ** -0.5
BIG = 3.0e38

FIRST, LAST = -1, PAIRS + 2
LOOP_FROM = 5
LOOP_N = PAIRS - 3 - LOOP_FROM
assert LOOP_N % 2 == 0

BANK_HEADS = [[b, b + HC, b + 2 * HC] for b in range(HC)]

A_USERS = (["wo_1", "xt0", "xt1", "v0_0", "pv1_1", "g0_0", "g0_1", "g0_2", "g1_0", "g1_1", "g1_2", "pv0_0", "v1_0"]
           + ["wo_0", "g0_3", "g0_4", "pv1_0", "v0_1", "g0_5", "g1_3", "g1_4", "g1_5", "pv0_1", "v1_1"])
T_USERS = (["t1_1_0", "t1_1_1", "t1_1_2", "ot_1", "x1t0", "x1t1", "t0_0_0", "t0_0_1", "t0_0_2"]
           + ["t1_0_0", "t1_0_1", "t1_0_2", "ot_0", "t0_1_0", "t0_1_1", "t0_1_2"])
assert len(A_USERS) % 2 == 0 and len(T_USERS) % 2 == 0
BANK = {name: i % 2 for i, name in enumerate(A_USERS)} | {name: 2 + i % 2 for i, name in enumerate(T_USERS)}


class Pair:

    def __init__(self, r, off):
        self.r, self.off = r, off
        self.parity = off % 2

    def plus(self, d):
        return Pair(self.r, self.off + d)

    def index(self):
        return self.r + self.off

    def count(self, per_graph, g, plus):
        fixed = per_graph * (2 * self.off + g) + plus
        assert isinstance(self.r, int) or fixed > 0
        value = 2 * per_graph * self.r + fixed
        return max(value, 0) if isinstance(value, int) else value

    def loads(self):
        fixed = 16 * (self.off // 2 + 1)
        assert isinstance(self.r, int) or fixed > 0
        value = 8 * self.r + fixed
        return max(value, 0) if isinstance(value, int) else value

    def valid(self):
        return not isinstance(self.r, int) or 0 <= self.r + self.off < PAIRS


def is_peeled(r, off, n):
    return isinstance(r, int) and r + off == n


def is_filling(r, off):
    return is_peeled(r, off, 0) or is_peeled(r, off, 1)


def iterations(eng, body, drain, after_loop=None):
    for n in range(FIRST, LOOP_FROM):
        body(0, n)
    with eng.Fori(0, LOOP_N // 2) as turn:
        for u in range(2):
            body(2 * turn, LOOP_FROM + u)
    if after_loop:
        after_loop()
    for n in range(LOOP_FROM + LOOP_N, LAST + 1):
        (body if n < PAIRS else drain)(LOOP_N, n - LOOP_N)


def build(nc, x, adj, wts, bv0, bo0, bq1, bk1, bv1, beta, out):
    with ExitStack() as ctx:
        def sb(name, shape, dt=F32):
            return ctx.enter_context(nc.sbuf_tensor(name, shape, dt))

        def bank(name):
            return ctx.enter_context(nc.psum_tensor(name, [P, 512], F32))

        def sem(name):
            return ctx.enter_context(nc.semaphore(name))

        def sems(name, n=2):
            return [sem(f"{name}_{i}") for i in range(n)]

        NW, NS = 7, 2
        WV0, WQ0, WK0, WO0, WQ1, WK1, WV1 = range(NW)
        w_stage = [sb(f"w_stage{i}", [P, C, D]) for i in range(NS)]
        w_hi = [sb(f"w_hi{i}", [P, C, D], F32R) for i in range(NW)]
        w_lo = [sb(f"w_lo{i}", [P, C, D], F32R) for i in range(NW)]
        ident = sb("ident", [P, P])
        bv_row = [sb("bv0_row", [P, D]), sb("bv1_row", [P, D])]
        bo_row = sb("bo_row", [P, D])
        bqk1 = sb("bqk1", [P, 2, C])
        bq1s = sb("bq1s", [P, C])
        beta_col = sb("beta_col", [P, 1])
        neg_half = sb("neg_half", [P, 1])
        x_in = [sb(f"x_in{b}", [P, 2, D]) for b in range(2)]
        x_bo = [sb(f"x_bo{b}", [P, 2, D]) for b in range(2)]
        adj0 = [sb(f"adj0_{b}", [P, 2, N]) for b in range(2)]
        adj1 = [sb(f"adj1_{b}", [P, 2, N]) for b in range(2)]
        bias = [[sb(f"bias{l}_{b}", [P, 2, N]) for b in range(2)] for l in range(2)]
        qT = [[sb(f"q{l}T_{b}", [P, C, G2]) for b in range(2)] for l in range(2)]
        kT = [[sb(f"k{l}T_{b}", [P, C, G2]) for b in range(2)] for l in range(2)]
        v = [[sb(f"v{l}_{b}", [P, 2, D]) for b in range(2)] for l in range(2)]
        x1 = [sb(f"x1_{b}", [P, 2, D]) for b in range(2)]
        x1_late = [sb(f"x1_late{b}", [P, 2, D]) for b in range(2)]
        xT_hi, xT_lo = sb("xT_hi", [P, C, G2], F32R), sb("xT_lo", [P, C, G2], F32R)
        x1T_hi, x1T_lo = sb("x1T_hi", [P, C, G2], F32R), sb("x1T_lo", [P, C, G2], F32R)
        neg_s = [sb(f"neg_s{l}", [P, H, N]) for l in range(2)]
        neg_max = [sb(f"neg_max{l}", [P, H]) for l in range(2)]
        prob = [sb(f"prob{l}", [P, H, N]) for l in range(2)]
        row_sum = [sb(f"row_sum{l}", [P, H]) for l in range(2)]
        inv_sum = [sb(f"inv_sum{l}", [P, H]) for l in range(2)]
        inv_raw0 = sb("inv_raw0", [P, H])
        abs_max0 = sb("abs_max0", [P, H])
        probT = [[sb(f"prob{l}T_{c}", [P, HC, N]) for c in range(C)] for l in range(2)]
        o0T_hi, o0T_lo = sb("o0T_hi", [P, C, N], F32R), sb("o0T_lo", [P, C, N], F32R)
        o1T = sb("o1T", [P, C, N])
        y = [sb(f"y{l}", [P, D]) for l in range(2)]
        stats = [sb(f"stats{l}", [P, 6]) for l in range(2)]
        mean_var = [sb(f"mean_var{l}", [P, 2]) for l in range(2)]
        var_eps = [sb(f"var_eps{l}", [P, 1]) for l in range(2)]
        rstd = [sb(f"rstd{l}", [P, 1]) for l in range(2)]
        mask1, linear1 = sb("mask1", [P, 2, N]), sb("linear1", [P, 2, N])
        x2 = [sb(f"x2_{g}", [P, D]) for g in range(2)]

        s_bank = [bank(f"s_bank{i}") for i in range(HC)]
        a_bank = [bank(f"a_bank{i}") for i in range(2)]
        t_bank = [bank(f"t_bank{i}") for i in range(2)]

        def ring(name):
            return (a_bank + t_bank)[BANK[name]]

        w_loaded = sems("w_loaded", NW)
        bv_loaded, small_loaded = sem("bv_loaded"), sem("small_loaded")
        x_loaded, adj0_loaded, adj1_loaded = sems("x_loaded"), sems("adj0_loaded"), sems("adj1_loaded")
        x1_kept = sems("x1_kept")
        stored = sems("stored")
        w_hi_done = sem("w_hi_done")
        w_lo_done = sems("w_lo_done", NW)
        const_done = sem("const_done")
        ident_done = sem("ident_done")
        dve_passed, pool_passed = sem("dve_passed"), sem("pool_passed")
        xt_done, x1t_done = sem("xt_done"), sem("x1t_done")
        g_done = sems("g_done")
        v_done = sems("v_done")
        s_done = sems("s_done")
        pt_done = sems("pt_done")
        pv_done = sems("pv_done")
        wo_done, ot_done = sem("wo_done"), sem("ot_done")
        xt_hi_done, x1t_hi_done, o0t_hi_done = sem("xt_hi_done"), sem("x1t_hi_done"), sem("o0t_hi_done")
        g_out = sems("g_out")
        exp_done = sems("exp_done")
        xt_lo_done, x1t_lo_done, o0t_lo_done = sem("xt_lo_done"), sem("x1t_lo_done"), sem("o0t_lo_done")
        v_out = sems("v_out")
        o1t_out = sem("o1t_out")
        neg_done = sems("neg_done")
        absmax_done = sem("absmax_done")
        inv0_steps = sem("inv0_steps")
        inv1_done = sem("inv1_done")
        y0_done, y1_att_done = sem("y0_done"), sem("y1_att_done")
        norm_stats = sems("norm_stats")
        x1_done, x2_done = sem("x1_done"), sem("x2_done")
        x_bo_done, bias0_done, bias1_steps = sem("x_bo_done"), sem("bias0_done"), sem("bias1_steps")
        rstd_steps = sems("rstd_steps")
        probn_done = sem("probn_done")
        y1_done = sem("y1_done")
        pt_out = [sems(f"pt{l}_out", C) for l in range(2)]

        block = ctx.enter_context(nc.Block())

        @block.sync
        def _(sp):
            def load_x(q):
                if q.valid():
                    b = q.parity
                    sp.wait_ge(xt_done, q.plus(-2).count(1, 1, 1))
                    sp.wait_ge(x_bo_done, q.plus(-2).count(1, 1, 1))
                    sp.dma_start(x_in[b][:], x[bass.ds(2 * q.index(), 2)].rearrange("g n d -> n g d")
                                 ).then_inc(x_loaded[b], 16)

            def load_adj0(q):
                if q.valid():
                    b = q.parity
                    sp.wait_ge(bias0_done, q.plus(-2).count(1, 1, 1))
                    sp.dma_start(adj0[b][:], adj[bass.ds(2 * q.index(), 2)].rearrange("g n k -> n g k")
                                 ).then_inc(adj0_loaded[b], 16)

            def load_adj1(q):
                if q.valid():
                    b = q.parity
                    sp.wait_ge(bias1_steps, q.plus(-2).count(5, 1, 5))
                    sp.dma_start(adj1[b][:], adj[bass.ds(2 * q.index(), 2)].rearrange("g n k -> n g k")
                                 ).then_inc(adj1_loaded[b], 16)

            def store(q, g):
                if q.valid():
                    sp.wait_ge(x2_done, q.count(1, g, 1))
                    sp.dma_start(out[bass.ds(2 * q.index() + g, 1)].rearrange("g n d -> n (g d)"), x2[g][:]
                                 ).then_inc(stored[g], 16)

            def keep_x1(q):
                if q.valid():
                    b = q.parity
                    sp.wait_ge(x1_done, q.count(1, 1, 1))
                    sp.wait_ge(y1_done, q.plus(-2).count(1, 1, 1))
                    sp.dma_start(x1_late[b][:], x1[b][:]).then_inc(x1_kept[b], 16)

            def load_weights(i):
                if i >= NS:
                    sp.wait_ge(w_lo_done[i - NS], 1)
                sp.dma_start(w_stage[i % NS][:], wts[i].rearrange("(c p) o -> p c o", p=P)
                             ).then_inc(w_loaded[i], 16)

            load_x(Pair(0, 0))
            load_weights(WV0)
            load_weights(WQ0)
            for layer, b_ in enumerate((bv0, bv1)):
                sp.dma_start(bv_row[layer][:], b_.partition_broadcast(P)).then_inc(bv_loaded, 16)
            load_adj0(Pair(0, 0))
            load_weights(WK0)
            sp.dma_start(bo_row[:], bo0.partition_broadcast(P)).then_inc(small_loaded, 16)
            load_weights(WO0)
            load_x(Pair(0, 1))
            load_adj0(Pair(0, 1))
            sp.dma_start(beta_col[:], beta.partition_broadcast(P)).then_inc(small_loaded, 16)
            for j, b_ in enumerate((bq1, bk1)):
                sp.dma_start(bqk1[:, j, :], b_.rearrange("(c p) -> p c", p=P),
                             allow_slow_non_contiguous=True).then_inc(small_loaded, 16)
            for i in (WQ1, WK1, WV1):
                load_weights(i)

            def body(r, off):
                n = Pair(r, off)
                load_x(n.plus(3))
                load_adj0(n.plus(3))
                store(n.plus(-3), 1)
                keep_x1(n.plus(-1))
                load_adj1(n.plus(1))
                store(n.plus(-2), 0)

            iterations(sp, body, body)
            for g in range(2):
                sp.wait_ge(stored[g], 16 * PAIRS)

        @block.tensor
        def _(pe):
            read = [(xt_lo_done, 0, 0, 0, 0)] * 4
            s_read = [(neg_done[0], 0, 0, 0, 0)] * HC

            def last_read(table, i, r):
                sem_, off, per, g, plus = table[i]
                return sem_, Pair(r, off).count(per, g, plus)

            def after_loop():
                for table in (read, s_read):
                    for i, (sem_, off, per, g, plus) in enumerate(table):
                        table[i] = (sem_, off - 2, per, g, plus)

            def transpose_x(q, g, r):
                if q.valid():
                    pe.wait_ge(*last_read(read, BANK[f"xt{g}"], r))
                    read[BANK[f"xt{g}"]] = (xt_lo_done, q.off, 1, g, 1)
                    pe.wait_ge(x_loaded[q.parity], q.loads())
                    for c in range(C):
                        mm = pe.transpose(ring(f"xt{g}")[:, c * P:(c + 1) * P],
                                          x_in[q.parity][:, g, c * P:(c + 1) * P], ident[:])
                    mm.then_inc(xt_done, 1)

            def transpose_x1(q, g, r):
                if q.valid():
                    pe.wait_ge(*last_read(read, BANK[f"x1t{g}"], r))
                    read[BANK[f"x1t{g}"]] = (x1t_lo_done, q.off, 1, g, 1)
                    pe.wait_ge(x1_done, q.count(1, g, 1))
                    for c in range(C):
                        mm = pe.transpose(ring(f"x1t{g}")[:, c * P:(c + 1) * P],
                                          x1[q.parity][:, g, c * P:(c + 1) * P], ident[:])
                    mm.then_inc(x1t_done, 1)

            def split_product(dst, a_hi, a_lo, b_hi, b_lo):
                for c in range(C):
                    pe.matmul(dst, a_hi(c), b_hi(c), start=(c == 0), stop=False)
                    pe.matmul(dst, a_hi(c), b_lo(c), start=False, stop=False)
                    mm = pe.matmul(dst, a_lo(c), b_hi(c), start=False, stop=(c == C - 1))
                return mm

            t_hi, t_lo = (xT_hi, x1T_hi), (xT_lo, x1T_lo)
            lo_done = (xt_lo_done, x1t_lo_done)

            def project_qk(layer, q, j, r):
                if q.valid():
                    name = f"g{layer}_{j}"
                    pe.wait_ge(*last_read(read, BANK[name], r))
                    read[BANK[name]] = (g_out[layer], q.off, 3, 0, j + 1)
                    pe.wait_ge(lo_done[layer], q.count(1, 1, 1))
                    wi = ((WQ0, WK0), (WQ1, WK1))[layer][j // C]
                    if is_peeled(r, q.off, 0):
                        pe.wait_ge(w_lo_done[wi], 1)
                    f = slice((j % C) * P, (j % C + 1) * P)
                    split_product(ring(name)[:, 0:G2], lambda c: w_hi[wi][:, c, f], lambda c: w_lo[wi][:, c, f],
                                  lambda c: t_hi[layer][:, c, :], lambda c: t_lo[layer][:, c, :]
                                  ).then_inc(g_done[layer], 1)

            def project_v(layer, q, g, r):
                if q.valid():
                    name = f"v{layer}_{g}"
                    pe.wait_ge(*last_read(read, BANK[name], r))
                    read[BANK[name]] = (v_out[layer], q.off, 1, g, 1)
                    wi = (WV0, WV1)[layer]
                    if is_peeled(r, q.off, 0):
                        pe.wait_ge(w_lo_done[wi], 1)
                    m = slice(g * N, (g + 1) * N)
                    split_product(ring(name)[:, 0:D], lambda c: t_hi[layer][:, c, m], lambda c: t_lo[layer][:, c, m],
                                  lambda c: w_hi[wi][:, c, :], lambda c: w_lo[wi][:, c, :]
                                  ).then_inc(v_done[layer], 1)

            def scores(layer, q, g, r):
                if q.valid():
                    pe.wait_ge(g_out[layer], q.count(3, 1, 3))
                    m = slice(g * N, (g + 1) * N)
                    for h in range(H):
                        c, j = divmod(h, HC)
                        if c == 0:
                            pe.wait_ge(*last_read(s_read, j, r))
                            s_read[j] = (neg_done[layer], q.off, H, g, C * (j + 1))
                        rows = slice(HD * j, HD * (j + 1))
                        mm = pe.matmul(s_bank[j][:, c * N:(c + 1) * N], qT[layer][q.parity][rows, c, m],
                                       kT[layer][q.parity][rows, c, m], start=True, stop=True)
                        if c == C - 1:
                            mm.then_inc(s_done[layer], 1)

            def transpose_probs(layer, q, g, c, r):
                if q.valid():
                    name = f"t{layer}_{g}_{c}"
                    pe.wait_ge(*last_read(read, BANK[name], r))
                    read[BANK[name]] = (pt_out[layer][c], q.off, 1, g, 1)
                    if layer == 0:
                        pe.wait_ge(probn_done, q.count(C, g, c + 1))
                    else:
                        pe.wait_ge(exp_done[1], q.count(H, g, H))
                    for j in range(HC):
                        mm = pe.transpose(ring(name)[:, j * N:(j + 1) * N], prob[layer][:, HC * c + j, :], ident[:])
                    mm.then_inc(pt_done[layer], 1)

            def attend(layer, q, g, r):
                if q.valid():
                    name = f"pv{layer}_{g}"
                    pe.wait_ge(*last_read(read, BANK[name], r))
                    read[BANK[name]] = ((o0t_lo_done, o1t_out)[layer], q.off, 1, g, 1)
                    pe.wait_ge(v_out[layer], q.count(1, g, 1))
                    for c in range(C):
                        pe.wait_ge(pt_out[layer][c], q.count(1, g, 1))
                        for j in range(HC):
                            f = slice(HD * (HC * c + j), HD * (HC * c + j + 1))
                            mm = pe.matmul(ring(name)[HD * j:HD * (j + 1), c * N:(c + 1) * N],
                                           v[layer][q.parity][:, g, f], probT[layer][c][:, j, :],
                                           start=True, stop=True)
                        mm.then_inc(pv_done[layer], 1)

            def transpose_out1(q, g, r):
                if q.valid():
                    name = f"ot_{g}"
                    pe.wait_ge(*last_read(read, BANK[name], r))
                    read[BANK[name]] = (y1_att_done, q.off, 1, g, 1)
                    pe.wait_ge(o1t_out, q.count(1, g, 1))
                    for c in range(C):
                        mm = pe.transpose(ring(name)[:, c * P:(c + 1) * P], o1T[:, c, :], ident[:])
                    mm.then_inc(ot_done, 1)

            def project_out0(q, g, r):
                if q.valid():
                    name = f"wo_{g}"
                    pe.wait_ge(*last_read(read, BANK[name], r))
                    read[BANK[name]] = (y0_done, q.off, 1, g, 1)
                    pe.wait_ge(o0t_lo_done, q.count(1, g, 1))
                    if is_peeled(r, q.off, 0):
                        pe.wait_ge(w_lo_done[WO0], 1)
                    split_product(ring(name)[:, 0:D], lambda c: o0T_hi[:, c, :], lambda c: o0T_lo[:, c, :],
                                  lambda c: w_hi[WO0][:, c, :], lambda c: w_lo[WO0][:, c, :]
                                  ).then_inc(wo_done, 1)

            pe.wait_ge(ident_done, 2)

            def body(r, off):
                n = Pair(r, off)
                nxt, prev, prev2, prev3 = n.plus(1), n.plus(-1), n.plus(-2), n.plus(-3)
                if not is_filling(r, off - 1):
                    scores(0, n, 0, r)
                project_out0(prev, 1, r)
                if not is_peeled(r, off, 0):
                    transpose_x(nxt, 0, r)
                transpose_probs(1, prev3, 1, 0, r)
                transpose_probs(1, prev3, 1, 1, r)
                if not is_peeled(r, off, 0):
                    transpose_x(nxt, 1, r)
                transpose_probs(1, prev3, 1, 2, r)
                project_v(0, nxt, 0, r)
                attend(1, prev3, 1, r)
                project_qk(0, nxt, 0, r)
                project_qk(0, nxt, 1, r)
                transpose_out1(prev3, 1, r)
                project_qk(0, nxt, 2, r)
                transpose_x1(prev, 0, r)
                transpose_x1(prev, 1, r)
                scores_and_layer1_part(n, prev, prev2, 0, r)
                if not is_filling(r, off):
                    scores(0, n, 1, r)
                project_out0(n, 0, r)
                transpose_probs(1, prev2, 0, 0, r)
                transpose_probs(1, prev2, 0, 1, r)
                project_qk(0, nxt, 3, r)
                transpose_probs(1, prev2, 0, 2, r)
                project_qk(0, nxt, 4, r)
                attend(1, prev2, 0, r)
                project_v(0, nxt, 1, r)
                project_qk(0, nxt, 5, r)
                transpose_out1(prev2, 0, r)
                scores_and_layer1_part(n, prev, prev2, 1, r)
                if is_peeled(r, off, -1):
                    transpose_x(nxt.plus(1), 0, r)
                    transpose_x(nxt.plus(1), 1, r)

            def scores_and_layer1_part(n, prev, prev2, g, r):
                if is_filling(r, n.off):
                    scores(0, n.plus(g), 1 - g, r)
                scores(1, prev2, g, r)
                project_qk(1, prev, 3 * g, r)
                transpose_probs(0, n, g, 0, r)
                transpose_probs(0, n, g, 1, r)
                project_qk(1, prev, 3 * g + 1, r)
                transpose_probs(0, n, g, 2, r)
                project_qk(1, prev, 3 * g + 2, r)
                attend(0, n, g, r)
                project_v(1, prev, g, r)

            def drain(r, off):
                n = Pair(r, off)
                prev, prev2 = n.plus(-1), n.plus(-2)
                project_out0(prev, 1, r)
                for g in range(2):
                    late = n.plus(-3 + g)
                    scores(1, prev2, g, r)
                    for c in range(C):
                        transpose_probs(1, late, 1 - g, c, r)
                    attend(1, late, 1 - g, r)
                    if g == 0:
                        transpose_x1(prev, 0, r)
                        transpose_x1(prev, 1, r)
                    transpose_out1(late, 1 - g, r)
                    for j in range(C):
                        project_qk(1, prev, C * g + j, r)
                    project_v(1, prev, g, r)

            iterations(pe, body, drain, after_loop)

        @block.scalar
        def _(act):
            def high_weights(*which):
                for i in which:
                    act.wait_ge(w_loaded[i], 16)
                    act.activation(w_hi[i][:], w_stage[i % NS][:], ACT.Copy).then_inc(w_hi_done, 1)

            def high_xT(q, g):
                if q.valid():
                    act.wait_ge(xt_done, q.count(1, g, 1))
                    if g == 0:
                        act.wait_ge(v_done[0], q.count(1, 0, 0))
                    act.activation(xT_hi[:, :, g * N:(g + 1) * N],
                                   ring(f"xt{g}")[:, 0:D].rearrange("p (c n) -> p c n", c=C), ACT.Copy
                                   ).then_inc(xt_hi_done, 1)

            def high_x1T(q, g):
                if q.valid():
                    act.wait_ge(x1t_done, q.count(1, g, 1))
                    if g == 0:
                        act.wait_ge(v_done[1], q.count(1, 0, 0))
                    act.activation(x1T_hi[:, :, g * N:(g + 1) * N],
                                   ring(f"x1t{g}")[:, 0:D].rearrange("p (c n) -> p c n", c=C), ACT.Copy
                                   ).then_inc(x1t_hi_done, 1)

            def high_o0T(q, g):
                if q.valid():
                    act.wait_ge(pv_done[0], q.count(C, g, C))
                    act.wait_ge(wo_done, q.count(1, g, 0))
                    act.activation(o0T_hi[:], ring(f"pv0_{g}")[:, 0:D].rearrange("p (c n) -> p c n", c=C),
                                   ACT.Copy).then_inc(o0t_hi_done, 1)

            def qk_out(layer, q, j, r):
                if q.valid():
                    b, c = q.parity, j % C
                    if layer == 1 and is_peeled(r, q.off, 0):
                        act.wait_ge(const_done, 2)
                        act.wait_ge(small_loaded, 16 * 4)
                    act.wait_ge(g_done[layer], q.count(3, 0, j + 1))
                    act.wait_ge(s_done[layer], q.plus(-2).count(HC, 1, HC))
                    src = ring(f"g{layer}_{j}")[:, 0:G2]
                    if layer == 0:
                        dst = (qT if j < C else kT)[0][b][:, c, :]
                        ins = act.activation(dst, src, ACT.Copy, scale=SCALE0 if j < C else 1.0)
                    elif j < C:
                        ins = act.activation(qT[1][b][:, c, :], src, ACT.Identity, bias=bq1s[:, c:c + 1], scale=SCALE1)
                    else:
                        ins = act.activation(kT[1][b][:, c, :], src, ACT.Identity, bias=bqk1[:, 1, c:c + 1])
                    ins.then_inc(g_out[layer], 1)

            def probT_out(layer, q, g, c):
                if q.valid():
                    act.wait_ge(pt_done[layer], q.count(C, g, c + 1))
                    act.wait_ge(pv_done[layer], q.count(C, g, c + 1 - C))
                    act.activation(probT[layer][c][:],
                                   ring(f"t{layer}_{g}_{c}")[:].rearrange("p (j n) -> p j n", j=HC), ACT.Copy
                                   ).then_inc(pt_out[layer][c], 1)

            def exps(layer, q, g, first, end):
                if q.valid():
                    if first == 0:
                        act.wait_ge(pt_done[layer], q.count(C, g, 0))
                        if layer == 1:
                            act.wait_ge(inv1_done, q.count(1, g, 0))
                    for i in range(first, end):
                        h = BANK_HEADS[i // C][i % C]
                        act.wait_ge(neg_done[layer], q.count(H, g, i + 1))
                        act.activation(prob[layer][:, h, :], neg_s[layer][:, h, :], ACT.Exp,
                                       bias=neg_max[layer][:, h:h + 1], scale=-1.0,
                                       accum_out=row_sum[layer][:, h:h + 1]).then_inc(exp_done[layer], 1)


            def body(r, off):
                n = Pair(r, off)
                nxt, prev, prev2, prev3 = n.plus(1), n.plus(-1), n.plus(-2), n.plus(-3)
                exps(0, n, 0, 0, 3)
                if not is_peeled(r, off, 0):
                    high_xT(nxt, 0)
                probT_out(1, prev3, 1, 0)
                if not is_peeled(r, off, 0):
                    high_xT(nxt, 1)
                if is_peeled(r, off, -1):
                    high_weights(WV0, WQ0, WK0)
                probT_out(1, prev3, 1, 2)
                exps(0, n, 0, 3, 10)
                qk_out(0, nxt, 0, r)
                exps(0, n, 0, 10, H)
                qk_out(0, nxt, 1, r)
                qk_out(0, nxt, 2, r)
                if is_peeled(r, off, -1):
                    high_weights(WO0)
                if is_peeled(r, off, 0):
                    high_weights(WK1)
                high_x1T(prev, 0)
                high_x1T(prev, 1)
                layer1_part(n, prev, prev2, 0, r)
                if is_peeled(r, off, 0):
                    high_weights(WV1)
                exps(0, n, 1, 0, 4)
                probT_out(1, prev2, 0, 0)
                exps(0, n, 1, 4, 6)
                qk_out(0, nxt, 3, r)
                probT_out(1, prev2, 0, 2)
                exps(0, n, 1, 6, 7)
                qk_out(0, nxt, 4, r)
                exps(0, n, 1, 7, H)
                qk_out(0, nxt, 5, r)
                layer1_part(n, prev, prev2, 1, r)
                if is_peeled(r, off, -1):
                    high_xT(nxt.plus(1), 0)
                    high_xT(nxt.plus(1), 1)
                    high_weights(WQ1)

            def layer1_part(n, prev, prev2, g, r):
                exps(1, prev2, g, 0, 2)
                qk_out(1, prev, 3 * g, r)
                probT_out(0, n, g, 0)
                exps(1, prev2, g, 2, 3)
                qk_out(1, prev, 3 * g + 1, r)
                probT_out(0, n, g, 2)
                exps(1, prev2, g, 3, 4)
                qk_out(1, prev, 3 * g + 2, r)
                exps(1, prev2, g, 4, 6)
                high_o0T(n, g)
                exps(1, prev2, g, 6, H)

            def drain(r, off):
                n = Pair(r, off)
                prev, prev2 = n.plus(-1), n.plus(-2)
                for g in range(2):
                    late = n.plus(-3 + g)
                    probT_out(1, late, 1 - g, 0)
                    probT_out(1, late, 1 - g, 2)
                    exps(1, prev2, g, 0, 2)
                    if g == 0:
                        high_x1T(prev, 0)
                        high_x1T(prev, 1)
                    for j in range(C):
                        exps(1, prev2, g, 2 + 2 * j, 4 + 2 * j)
                        qk_out(1, prev, C * g + j, r)
                    exps(1, prev2, g, 8, H)

            iterations(act, body, drain)

        @block.vector
        def _(dve):
            def low_weights(*which):
                for i in which:
                    dve.wait_ge(w_hi_done, i + 1)
                    dve.tensor_tensor(w_lo[i][:], w_stage[i % NS][:], w_hi[i][:].bitcast(F32), ALU.subtract
                                      ).then_inc(w_lo_done[i], 1)

            def add_residual0(q, g):
                if q.valid():
                    dve.wait_ge(wo_done, q.count(1, g, 1))
                    dve.wait_ge(x_bo_done, q.count(1, 1, 1))
                    dve.wait_ge(x1_done, q.count(1, g, 0))
                    dve.tensor_tensor(y[0][:], ring(f"wo_{g}")[:, 0:D], x_bo[q.parity][:, g, :], ALU.add
                                      ).then_inc(y0_done, 1)

            def norm_input0(q, g):
                if q.valid():
                    dve.wait_ge(y0_done, q.count(1, g, 1))
                    norm_stats_of(0, q, g)

            def norm_stats_of(layer, q, g):
                dve.bn_stats(stats[layer][:], y[layer][:]).then_inc(norm_stats[layer], 1)
                dve.wait_ge(norm_stats[layer], q.count(2, g, 1))
                dve.sem_inc(dve_passed, 1)
                dve.bn_aggr(mean_var[layer][:], stats[layer][:]).then_inc(norm_stats[layer], 1)

            def norm_apply0(q, g):
                if q.valid():
                    dve.wait_ge(rstd_steps[0], q.count(2, g, 2))
                    dve.wait_ge(x1t_done, q.plus(-2).count(1, g, 1))
                    dve.wait_ge(x1_kept[q.parity], q.plus(-2).loads())
                    dve.tensor_scalar(x1[q.parity][:, g, :], y[0][:], mean_var[0][:, 0:1], rstd[0][:],
                                      ALU.subtract, ALU.mult).then_inc(x1_done, 1)

            def negate(layer, q, g, banks):
                if q.valid():
                    for b in banks:
                        if b == 0:
                            if layer == 0:
                                dve.wait_ge(bias0_done, q.count(1, 1, 1))
                                dve.wait_ge(absmax_done, q.count(1, g, 0))
                            else:
                                dve.wait_ge(bias1_steps, q.count(5, 1, 5))
                            dve.wait_ge(exp_done[layer], q.count(H, g, 0))
                        dve.wait_ge(s_done[layer], q.count(HC, g, b + 1))
                        dve.sem_inc(dve_passed, 1)
                        for h in BANK_HEADS[b]:
                            dve.tensor_tensor_reduce(neg_s[layer][:, h, :],
                                                     s_bank[b][:, (h // HC) * N:(h // HC + 1) * N],
                                                     bias[layer][q.parity][:, g, :], -1.0, BIG, ALU.add, ALU.min,
                                                     neg_max[layer][:, h:h + 1]).then_inc(neg_done[layer], 1)

            def probT_out(layer, q, g):
                if q.valid():
                    dve.wait_ge(pt_done[layer], q.count(C, g, 2))
                    dve.wait_ge(pv_done[layer], q.count(C, g, 2 - C))
                    dve.tensor_copy(probT[layer][1][:],
                                    ring(f"t{layer}_{g}_1")[:].rearrange("p (j n) -> p j n", j=HC)
                                    ).then_inc(pt_out[layer][1], 1)

            def low_part(dst, name, hi, hi_done, done, q, g):
                dve.wait_ge(hi_done, q.count(1, g, 1))
                dve.tensor_tensor(dst, ring(name)[:, 0:D].rearrange("p (c n) -> p c n", c=C), hi.bitcast(F32),
                                  ALU.subtract).then_inc(done, 1)

            def low_xT(q, g):
                if q.valid():
                    if g == 0:
                        dve.wait_ge(v_done[0], q.count(1, 0, 0))
                    m = slice(g * N, (g + 1) * N)
                    low_part(xT_lo[:, :, m], f"xt{g}", xT_hi[:, :, m], xt_hi_done, xt_lo_done, q, g)

            def low_x1T(q, g):
                if q.valid():
                    if g == 0:
                        dve.wait_ge(v_done[1], q.count(1, 0, 0))
                    m = slice(g * N, (g + 1) * N)
                    low_part(x1T_lo[:, :, m], f"x1t{g}", x1T_hi[:, :, m], x1t_hi_done, x1t_lo_done, q, g)

            def low_o0T(q, g):
                if q.valid():
                    dve.wait_ge(wo_done, q.count(1, g, 0))
                    low_part(o0T_lo[:], f"pv0_{g}", o0T_hi[:], o0t_hi_done, o0t_lo_done, q, g)

            def out1T_out(q, g):
                if q.valid():
                    dve.wait_ge(pv_done[1], q.count(C, g, C))
                    dve.wait_ge(ot_done, q.count(1, g, 0))
                    dve.tensor_copy(o1T[:], ring(f"pv1_{g}")[:, 0:D].rearrange("p (c n) -> p c n", c=C)
                                    ).then_inc(o1t_out, 1)

            def abs_max(q, g):
                if q.valid():
                    dve.wait_ge(neg_done[0], q.count(H, g, H))
                    dve.wait_ge(inv0_steps, q.count(2, g, 0))
                    dve.tensor_reduce(abs_max0[:], neg_s[0][:], AX_X, ALU.max, apply_absolute_value=True
                                      ).then_inc(absmax_done, 1)

            def inverse_sums1(q, g):
                if q.valid():
                    dve.wait_ge(exp_done[1], q.count(H, g, H))
                    dve.wait_ge(y1_att_done, q.count(1, g, 0))
                    dve.reciprocal(inv_sum[1][:], row_sum[1][:]).then_inc(inv1_done, 1)

            def attention_out1(q, g):
                if q.valid():
                    dve.wait_ge(ot_done, q.count(1, g, 1))
                    dve.wait_ge(inv1_done, q.count(1, g, 1))
                    dve.wait_ge(x2_done, q.count(1, g, 0))
                    dve.tensor_tensor(y[1][:].rearrange("p (h e) -> p h e", h=H),
                                      ring(f"ot_{g}")[:, 0:D].rearrange("p (h e) -> p h e", h=H),
                                      inv_sum[1][:].unsqueeze(2).to_broadcast([P, H, HD]), ALU.mult
                                      ).then_inc(y1_att_done, 1)

            def values_out(layer, q, g):
                if q.valid():
                    if is_peeled(q.r, q.off, 0):
                        dve.wait_ge(bv_loaded, 16 * 2)
                    dve.wait_ge(v_done[layer], q.count(1, g, 1))
                    dve.wait_ge(pv_done[layer], q.plus(-2).count(C, g, C))
                    dve.tensor_tensor(v[layer][q.parity][:, g, :], ring(f"v{layer}_{g}")[:, 0:D], bv_row[layer][:],
                                      ALU.add).then_inc(v_out[layer], 1)

            def inverse_sums0(q, g):
                if q.valid():
                    dve.wait_ge(exp_done[0], q.count(H, g, H))
                    dve.reciprocal(inv_raw0[:], row_sum[0][:]).then_inc(inv0_steps, 1)
                    dve.wait_ge(absmax_done, q.count(1, g, 1))
                    dve.wait_ge(probn_done, q.count(C, g, 0))
                    dve.wait_ge(inv0_steps, q.count(2, g, 1))
                    dve.scalar_tensor_tensor(out=inv_sum[0][:], in0=abs_max0[:], scalar=0.0, in1=inv_raw0[:],
                                             op0=ALU.is_gt, op1=ALU.mult).then_inc(inv0_steps, 1)

            def norm_input1(q, g):
                if q.valid():
                    dve.wait_ge(y1_done, q.count(1, g, 1))
                    norm_stats_of(1, q, g)

            def norm_apply1(q, g):
                if q.valid():
                    dve.wait_ge(rstd_steps[1], q.count(2, g, 2))
                    dve.wait_ge(stored[g], q.count(8, 0, 0))
                    dve.tensor_scalar(x2[g][:], y[1][:], mean_var[1][:, 0:1], rstd[1][:],
                                      ALU.subtract, ALU.mult).then_inc(x2_done, 1)

            def body(r, off):
                n = Pair(r, off)
                nxt, prev, prev2, prev3 = n.plus(1), n.plus(-1), n.plus(-2), n.plus(-3)
                if not is_filling(r, off - 1):
                    negate(0, n, 0, (0, 1, 2))
                add_residual0(prev, 1)
                if not is_filling(r, off - 1):
                    negate(0, n, 0, (3,))
                if not is_peeled(r, off, 0):
                    low_xT(nxt, 0)
                probT_out(1, prev3, 1)
                if not is_peeled(r, off, 0):
                    low_xT(nxt, 1)
                norm_input0(prev, 1)
                if is_peeled(r, off, -1):
                    low_weights(WV0, WQ0)
                values_out(0, nxt, 0)
                if is_peeled(r, off, -1):
                    low_weights(WK0)
                out1T_out(prev3, 1)
                norm_apply0(prev, 1)
                inverse_sums1(prev3, 1)
                abs_max(n, 0)
                attention_out1(prev3, 1)
                inverse_sums0(n, 0)
                low_x1T(prev, 0)
                low_x1T(prev, 1)
                layer1_part(n, prev, prev2, prev3, 0)
                if not is_filling(r, off):
                    negate(0, n, 1, (0, 1, 2, 3))
                add_residual0(n, 0)
                probT_out(1, prev2, 0)
                norm_input0(n, 0)
                norm_apply0(n, 0)
                out1T_out(prev2, 0)
                if is_filling(r, off):
                    abs_max(n, 1)
                values_out(0, nxt, 1)
                if not is_filling(r, off):
                    abs_max(n, 1)
                inverse_sums1(prev2, 0)
                inverse_sums0(n, 1)
                attention_out1(prev2, 0)
                layer1_part(n, prev, prev2, prev2, 1)
                if is_peeled(r, off, -1):
                    low_xT(nxt.plus(1), 0)
                    low_xT(nxt.plus(1), 1)

            def layer1_part(n, prev, prev2, late, g):
                if is_filling(n.r, n.off):
                    negate(0, n.plus(g), 1 - g, (0, 1, 2, 3))
                negate(1, prev2, g, (0, 1, 2, 3))
                probT_out(0, n, g)
                norm_input1(late, 1 - g)
                low_o0T(n, g)
                norm_apply1(late, 1 - g)
                values_out(1, prev, g)

            def drain(r, off):
                n = Pair(r, off)
                prev, prev2 = n.plus(-1), n.plus(-2)
                add_residual0(prev, 1)
                norm_input0(prev, 1)
                for g in range(2):
                    late = n.plus(-3 + g)
                    inverse_sums1(late, 1 - g)
                    negate(1, prev2, g, (0,))
                    if g == 0:
                        norm_apply0(prev, 1)
                    probT_out(1, late, 1 - g)
                    negate(1, prev2, g, (1, 2, 3))
                    if g == 0:
                        low_x1T(prev, 0)
                        low_x1T(prev, 1)
                    out1T_out(late, 1 - g)
                    attention_out1(late, 1 - g)
                    norm_input1(late, 1 - g)
                    norm_apply1(late, 1 - g)
                    values_out(1, prev, g)

            iterations(dve, body, drain)

        @block.gpsimd
        def _(pool):
            pool.memset(neg_half[:], -0.5).then_inc(const_done, 1)
            pool.memset(ident[:], 0.0).then_inc(ident_done, 1)
            pool.wait_ge(ident_done, 1)
            pool.affine_select(out=ident[:], in_=ident[:], compare_op=ALU.not_equal, fill=1.0, base=0,
                               pattern=[[-1, P]], channel_multiplier=1).then_inc(ident_done, 1)

            def low_weights(*which):
                for i in which:
                    pool.wait_ge(w_hi_done, i + 1)
                    pool.tensor_tensor(w_lo[i][:], w_stage[i % NS][:], w_hi[i][:].bitcast(F32), ALU.subtract
                                       ).then_inc(w_lo_done[i], 1)

            def inverse_std(layer, q, g):
                if q.valid():
                    pool.wait_ge(norm_stats[layer], q.count(2, g, 2))
                    pool.wait_ge((x1_done, x2_done)[layer], q.count(1, g, 0))
                    pool.wait_ge(rstd_steps[layer], q.count(2, g, 0))
                    pool.sem_inc(pool_passed, 1)
                    pool.tensor_scalar(var_eps[layer][:], mean_var[layer][:, 1:2], EPS, None, ALU.add
                                       ).then_inc(rstd_steps[layer], 1)
                    pool.wait_ge(rstd_steps[layer], q.count(2, g, 1))
                    pool.tensor_tensor(rstd[layer][:], var_eps[layer][:], neg_half[:], ALU.pow
                                       ).then_inc(rstd_steps[layer], 1)

            def residual0(q, r):
                if q.valid():
                    b = q.parity
                    if is_peeled(r, q.off, 0):
                        pool.wait_ge(small_loaded, 16 * 4)
                        pool.wait_ge(const_done, 1)
                    pool.wait_ge(x_loaded[b], q.loads())
                    pool.wait_ge(y0_done, q.plus(-2).count(1, 1, 1))
                    for g in range(2):
                        pool.tensor_tensor(x_bo[b][:, g, :], x_in[b][:, g, :], bo_row[:], ALU.add
                                           ).then_inc(x_bo_done, 1)

            def make_bias0(q):
                if q.valid():
                    b = q.parity
                    pool.wait_ge(adj0_loaded[b], q.loads())
                    pool.wait_ge(neg_done[0], q.plus(-2).count(H, 1, H))
                    for g in range(2):
                        pool.tensor_tensor(bias[0][b][:, g, :], adj0[b][:, g, :], adj0[b][:, g, :], ALU.add
                                           ).then_inc(bias0_done, 1)

            def make_bias1(q):
                if q.valid():
                    b = q.parity
                    pool.wait_ge(adj1_loaded[b], q.loads())
                    pool.wait_ge(neg_done[1], q.plus(-2).count(H, 1, H))
                    pool.wait_ge(bias1_steps, q.count(5, 0, 0))
                    pool.sem_inc(pool_passed, 1)
                    for g in range(2):
                        pool.tensor_scalar(mask1[:, g, :], adj1[b][:, g, :], 0.0, None, ALU.is_gt
                                           ).then_inc(bias1_steps, 1)
                    for g in range(2):
                        pool.tensor_scalar(linear1[:, g, :], adj1[b][:, g, :], beta_col[:], None, ALU.mult
                                           ).then_inc(bias1_steps, 1)
                    pool.wait_ge(bias1_steps, q.count(5, 0, 4))
                    for g in range(2):
                        pool.tensor_tensor(linear1[:, g, :], linear1[:, g, :], mask1[:, g, :], ALU.mult
                                           ).then_inc(bias1_steps, 1)
                    pool.wait_ge(bias1_steps, q.count(5, 0, 6))
                    pool.sem_inc(pool_passed, 1)
                    for g in range(2):
                        pool.tensor_scalar(mask1[:, g, :], mask1[:, g, :], 1.0, MASKED, ALU.subtract, ALU.mult
                                           ).then_inc(bias1_steps, 1)
                    pool.wait_ge(bias1_steps, q.count(5, 0, 8))
                    for g in range(2):
                        pool.tensor_tensor(bias[1][b][:, g, :], linear1[:, g, :], mask1[:, g, :], ALU.add
                                           ).then_inc(bias1_steps, 1)

            def residual1(q, g):
                if q.valid():
                    pool.wait_ge(y1_att_done, q.count(1, g, 1))
                    pool.wait_ge(x1_kept[q.parity], q.loads())
                    pool.tensor_tensor(y[1][:], y[1][:], x1_late[q.parity][:, g, :], ALU.add
                                       ).then_inc(y1_done, 1)

            def normalise0(q, g):
                if q.valid():
                    pool.wait_ge(inv0_steps, q.count(2, g, 2))
                    for c in range(C):
                        hs = slice(HC * c, HC * (c + 1))
                        pool.tensor_tensor(prob[0][:, hs, :], prob[0][:, hs, :],
                                           inv_sum[0][:, hs].unsqueeze(2).to_broadcast([P, HC, N]), ALU.mult
                                           ).then_inc(probn_done, 1)

            def body(r, off):
                n = Pair(r, off)
                nxt, prev, prev2 = n.plus(1), n.plus(-1), n.plus(-2)
                if is_peeled(r, off, 0):
                    pool.wait_ge(small_loaded, 16 * 4)
                    pool.tensor_scalar(bq1s[:], bqk1[:, 0, :], SCALE1, None, ALU.mult).then_inc(const_done, 1)
                for s in range(2):
                    late0, late1, lg = (prev, n.plus(-3), 1) if s == 0 else (n, prev2, 0)
                    inverse_std(0, late0, lg)
                    if s == 0:
                        residual0(nxt, r)
                        make_bias0(nxt)
                    normalise0(n, s)
                    if is_peeled(r, off, -1):
                        low_weights((WO0, WQ1)[s])
                    if is_peeled(r, off, 0):
                        low_weights((WK1, WV1)[s])
                    residual1(late1, lg)
                    inverse_std(1, late1, lg)
                    if s == 1:
                        make_bias1(prev)

            iterations(pool, body, body)


_WEIGHTS = ["L0_gnn_Wv", "L0_gnn_Wq", "L0_gnn_Wk", "L0_gnn_Wo", "L1_gnn_Wq", "L1_gnn_Wk", "L1_gnn_Wv"]
_VECTORS = ["L0_gnn_bv", "L0_gnn_bo", "L1_gnn_bq", "L1_gnn_bk", "L1_gnn_bv", "L1_gnn_beta"]


def kernel(**inputs):
    import numpy as _np
    import concourse.bacc as _bacc
    from concourse import mybir as _mybir
    from concourse.bass_utils import run_bass_kernel_spmd as _run

    nc = _bacc.Bacc("TRN2", target_bir_lowering=False, num_devices=1)
    arrays = {}

    def dram(name, a):
        a = _np.ascontiguousarray(a)
        arrays[f"in_{name}_dram"] = a
        return nc.dram_tensor(f"in_{name}_dram", a.shape, _mybir.dt.from_np(a.dtype), kind="ExternalInput").ap()

    x, adj = dram("x", inputs["x"]), dram("adj", inputs["adj"])
    wts = [dram(w, inputs[w].T if w.startswith("L0") else inputs[w]) for w in _WEIGHTS]
    bv0, bo0, bq1, bk1, bv1, beta = (dram(b, _np.reshape(inputs[b], (-1,))) for b in _VECTORS)
    out = nc.dram_tensor("out_0_dram", (128, 128, 384), _mybir.dt.float32, kind="ExternalOutput").ap()
    build(nc, x, adj, wts, bv0, bo0, bq1, bk1, bv1, beta, out)
    r = _run(nc, [arrays], core_ids=[0])
    return r.results[0]["out_0_dram"]
```
